# Optimizing a Trainium2 kernel written in Bass

```python
import numpy as np
import jax
import jax.numpy as jnp

def _softmax(x, axis=-1):
    return jax.nn.softmax(x, axis=axis)

def _gelu(x):
    return jax.nn.gelu(x, approximate=True)

def _silu(x):
    return jax.nn.silu(x)

def _sigmoid(x):
    return jax.nn.sigmoid(x)

def _layernorm(x, axis=-1, eps=1e-05):
    m = jnp.mean(x, axis=axis, keepdims=True)
    v = jnp.var(x, axis=axis, keepdims=True)
    return (x - m) / jnp.sqrt(v + eps)

def _scatter_add(tgt, idx, src, axis=0):
    return tgt.at[idx].add(src)

def _segment_sum(src, seg, n):
    return jax.ops.segment_sum(src, seg, n)
kernel_name = 'mk_seq_postln_d2_jaxref_r8_f91cd5'

def setup_inputs(seed: int=0):
    np.random.seed(seed)
    _w = jnp.asarray

    def _L0_attn_setup():
        import jax, jax.numpy as jnp
        import numpy as np
        D_INNER, D_STATE, DT_RANK = (256, 16, 128)
        BATCH, SEQ = (2, 256)

        def _selective_scan(u, delta, A, B, C, D):
            dA = jnp.exp(delta[..., None] * A[None, None])
            dBu = (delta * u)[..., None] * B[:, :, None, :]

            def step(h, inp):
                dA_t, dBu_t, C_t = inp
                h = dA_t * h + dBu_t
                y_t = jnp.einsum('bdn,bn->bd', h, C_t)
                return (h, y_t)
            h0 = jnp.zeros((u.shape[0], u.shape[2], A.shape[1]), dtype=u.dtype)
            xs = (jnp.moveaxis(dA, 1, 0), jnp.moveaxis(dBu, 1, 0), jnp.moveaxis(C, 1, 0))
            _, ys = jax.lax.scan(step, h0, xs)
            y = jnp.moveaxis(ys, 0, 1)
            return y + u * D[None, None, :]
        key = jax.random.key(seed)
        ks = jax.random.split(key, 6)
        x = jax.random.normal(ks[0], (BATCH, SEQ, D_INNER), dtype=jnp.float32)
        A_log = jax.random.uniform(ks[1], (D_INNER, D_STATE), minval=-4.0, maxval=-1.0, dtype=jnp.float32)
        D = jnp.ones((D_INNER,), dtype=jnp.float32)
        x_proj_w = jax.random.normal(ks[2], (DT_RANK + 2 * D_STATE, D_INNER), dtype=jnp.float32) / np.sqrt(D_INNER)
        dt_proj_w = jax.random.normal(ks[3], (D_INNER, DT_RANK), dtype=jnp.float32) / np.sqrt(DT_RANK)
        dt_std = DT_RANK ** (-0.5)
        dt_proj_b = jax.random.uniform(ks[4], (D_INNER,), minval=-dt_std, maxval=dt_std, dtype=jnp.float32)
        return {'x': x, 'A_log': A_log, 'D': D, 'x_proj_w': x_proj_w, 'dt_proj_w': dt_proj_w, 'dt_proj_b': dt_proj_b}
    _L0_attn_in = _L0_attn_setup()

    def _L0_ffn_setup():
        import jax, jax.numpy as jnp
        import numpy as np
        D_MODEL = 256
        D_EXPERT = 1024
        EPS = 1e-08

        def ternary_quant(w):
            scale = jnp.mean(jnp.abs(w)) + EPS
            q = jnp.clip(jnp.round(w / scale), -1.0, 1.0) * scale
            return w + jax.lax.stop_gradient(q - w)
        key = jax.random.key(seed)
        k_x, k_up, k_gate, k_down = jax.random.split(key, 4)
        std_in = 1.0 / np.sqrt(D_MODEL)
        std_exp = 1.0 / np.sqrt(D_EXPERT)
        return {'x': jax.random.normal(k_x, (4, 256, D_MODEL), dtype=jnp.float32), 'W_up': jax.random.normal(k_up, (D_EXPERT, D_MODEL), dtype=jnp.float32) * std_in, 'W_gate': jax.random.normal(k_gate, (D_EXPERT, D_MODEL), dtype=jnp.float32) * std_in, 'W_down': jax.random.normal(k_down, (D_MODEL, D_EXPERT), dtype=jnp.float32) * std_exp}
    _L0_ffn_in = _L0_ffn_setup()

    def _L1_attn_setup():
        import jax, jax.numpy as jnp
        import numpy as np
        EMBED_DIM = 256
        NUM_HEADS = 16
        HEAD_DIM = EMBED_DIM // NUM_HEADS
        WINDOW = 64
        CHUNK = WINDOW
        SCALE = 1.0 / float(np.sqrt(HEAD_DIM))

        def _sliding_window_attention(q, k, v):
            B, H, S, D = q.shape
            C = CHUNK
            nc = S // C
            qc = q.reshape(B, H, nc, C, D)
            kp = jnp.pad(k, ((0, 0), (0, 0), (C, 0), (0, 0))).reshape(B, H, nc + 1, C, D)
            vp = jnp.pad(v, ((0, 0), (0, 0), (C, 0), (0, 0))).reshape(B, H, nc + 1, C, D)
            kc = jnp.concatenate([kp[:, :, :-1], kp[:, :, 1:]], axis=-2)
            vc = jnp.concatenate([vp[:, :, :-1], vp[:, :, 1:]], axis=-2)
            qa = jnp.arange(C)
            ka = jnp.arange(2 * C)
            diff = C + qa[:, None] - ka[None, :]
            base = (diff >= 0) & (diff <= WINDOW)
            kv_pos = (jnp.arange(nc)[:, None] - 1) * C + ka[None, :]
            mask = base[None, :, :] & (kv_pos >= 0)[:, None, :]
            scores = jnp.einsum('bhncd,bhnkd->bhnck', qc, kc) * SCALE
            scores = jnp.where(mask[None, None], scores, -jnp.inf)
            attn = jax.nn.softmax(scores, axis=-1)
            out = jnp.einsum('bhnck,bhnkd->bhncd', attn, vc)
            return out.reshape(B, H, S, D)
        key = jax.random.key(seed)
        k1, k2, k3 = jax.random.split(key, 3)
        B, S, E = (2, 512, EMBED_DIM)
        x = jax.random.normal(k1, (B, S, E), dtype=jnp.float32)
        w_qkv = jax.random.normal(k2, (3 * E, E), dtype=jnp.float32) * (1.0 / np.sqrt(E))
        w_out = jax.random.normal(k3, (E, E), dtype=jnp.float32) * (1.0 / np.sqrt(E))
        return {'x': x, 'w_qkv': w_qkv, 'w_out': w_out}
    _L1_attn_in = _L1_attn_setup()

    def _L1_ffn_setup():
        import jax, jax.numpy as jnp
        import numpy as np
        DIM_IN = 256
        DIM_HIDDEN = 1024
        key = jax.random.key(seed)
        k_x, k_g, k_u, k_d = jax.random.split(key, 4)
        s_in = 1.0 / np.sqrt(DIM_IN)
        s_hid = 1.0 / np.sqrt(DIM_HIDDEN)
        x = jax.random.normal(k_x, (4, 256, DIM_IN), dtype=jnp.float32)
        w_gate = jax.random.uniform(k_g, (DIM_HIDDEN, DIM_IN), jnp.float32, -s_in, s_in)
        w_up = jax.random.uniform(k_u, (DIM_HIDDEN, DIM_IN), jnp.float32, -s_in, s_in)
        w_down = jax.random.uniform(k_d, (DIM_IN, DIM_HIDDEN), jnp.float32, -s_hid, s_hid)
        return {'x': x, 'w_gate': w_gate, 'w_up': w_up, 'w_down': w_down}
    _L1_ffn_in = _L1_ffn_setup()
    _d = {'L0_attn_x': _L0_attn_in['x'], 'L0_attn_A_log': _L0_attn_in['A_log'], 'L0_attn_D': _L0_attn_in['D'], 'L0_attn_x_proj_w': _L0_attn_in['x_proj_w'], 'L0_attn_dt_proj_w': _L0_attn_in['dt_proj_w'], 'L0_attn_dt_proj_b': _L0_attn_in['dt_proj_b'], 'L0_ffn_W_up': _L0_ffn_in['W_up'], 'L0_ffn_W_gate': _L0_ffn_in['W_gate'], 'L0_ffn_W_down': _L0_ffn_in['W_down'], 'L1_attn_w_qkv': _L1_attn_in['w_qkv'], 'L1_attn_w_out': _L1_attn_in['w_out'], 'L1_ffn_w_gate': _L1_ffn_in['w_gate'], 'L1_ffn_w_up': _L1_ffn_in['w_up'], 'L1_ffn_w_down': _L1_ffn_in['w_down']}
    _x0 = _d['L0_attn_x']
    _d['L0_attn_x'] = jax.random.normal(jax.random.fold_in(jax.random.key(seed), 1), (16, 256, 256), dtype=_x0.dtype)
    del _x0
    return _d

def reference(L0_attn_x, L0_attn_A_log, L0_attn_D, L0_attn_x_proj_w, L0_attn_dt_proj_w, L0_attn_dt_proj_b, L0_ffn_W_up, L0_ffn_W_gate, L0_ffn_W_down, L1_attn_w_qkv, L1_attn_w_out, L1_ffn_w_gate, L1_ffn_w_up, L1_ffn_w_down):

    def _L0_attn_ref(x, A_log, D, x_proj_w, dt_proj_w, dt_proj_b):
        import jax, jax.numpy as jnp
        import numpy as np
        D_INNER, D_STATE, DT_RANK = (256, 16, 128)
        BATCH, SEQ = (2, 256)

        def _selective_scan(u, delta, A, B, C, D):
            dA = jnp.exp(delta[..., None] * A[None, None])
            dBu = (delta * u)[..., None] * B[:, :, None, :]

            def step(h, inp):
                dA_t, dBu_t, C_t = inp
                h = dA_t * h + dBu_t
                y_t = jnp.einsum('bdn,bn->bd', h, C_t)
                return (h, y_t)
            h0 = jnp.zeros((u.shape[0], u.shape[2], A.shape[1]), dtype=u.dtype)
            xs = (jnp.moveaxis(dA, 1, 0), jnp.moveaxis(dBu, 1, 0), jnp.moveaxis(C, 1, 0))
            _, ys = jax.lax.scan(step, h0, xs)
            y = jnp.moveaxis(ys, 0, 1)
            return y + u * D[None, None, :]
        x_dbl = jnp.einsum('bld,ed->ble', x, x_proj_w)
        delta_r = x_dbl[..., :DT_RANK]
        B = x_dbl[..., DT_RANK:DT_RANK + D_STATE]
        C = x_dbl[..., DT_RANK + D_STATE:]
        delta = jnp.einsum('blr,dr->bld', delta_r, dt_proj_w) + dt_proj_b
        delta = jax.nn.softplus(delta)
        A = -jnp.exp(A_log)
        return _selective_scan(x, delta, A, B, C, D)

    def _L0_ffn_ref(x, W_up, W_gate, W_down):
        import jax, jax.numpy as jnp
        import numpy as np
        D_MODEL = 256
        D_EXPERT = 1024
        EPS = 1e-08

        def ternary_quant(w):
            scale = jnp.mean(jnp.abs(w)) + EPS
            q = jnp.clip(jnp.round(w / scale), -1.0, 1.0) * scale
            return w + jax.lax.stop_gradient(q - w)
        wu = ternary_quant(W_up)
        wg = ternary_quant(W_gate)
        wd = ternary_quant(W_down)
        up = jnp.einsum('bsd,ed->bse', x, wu)
        gate = jnp.einsum('bsd,ed->bse', x, wg)
        hidden = jax.nn.silu(up) * gate
        return jnp.einsum('bse,de->bsd', hidden, wd)

    def _L1_attn_ref(x, w_qkv, w_out):
        import jax, jax.numpy as jnp
        import numpy as np
        EMBED_DIM = 256
        NUM_HEADS = 16
        HEAD_DIM = EMBED_DIM // NUM_HEADS
        WINDOW = 64
        CHUNK = WINDOW
        SCALE = 1.0 / float(np.sqrt(HEAD_DIM))

        def _sliding_window_attention(q, k, v):
            B, H, S, D = q.shape
            C = CHUNK
            nc = S // C
            qc = q.reshape(B, H, nc, C, D)
            kp = jnp.pad(k, ((0, 0), (0, 0), (C, 0), (0, 0))).reshape(B, H, nc + 1, C, D)
            vp = jnp.pad(v, ((0, 0), (0, 0), (C, 0), (0, 0))).reshape(B, H, nc + 1, C, D)
            kc = jnp.concatenate([kp[:, :, :-1], kp[:, :, 1:]], axis=-2)
            vc = jnp.concatenate([vp[:, :, :-1], vp[:, :, 1:]], axis=-2)
            qa = jnp.arange(C)
            ka = jnp.arange(2 * C)
            diff = C + qa[:, None] - ka[None, :]
            base = (diff >= 0) & (diff <= WINDOW)
            kv_pos = (jnp.arange(nc)[:, None] - 1) * C + ka[None, :]
            mask = base[None, :, :] & (kv_pos >= 0)[:, None, :]
            scores = jnp.einsum('bhncd,bhnkd->bhnck', qc, kc) * SCALE
            scores = jnp.where(mask[None, None], scores, -jnp.inf)
            attn = jax.nn.softmax(scores, axis=-1)
            out = jnp.einsum('bhnck,bhnkd->bhncd', attn, vc)
            return out.reshape(B, H, S, D)
        B, S, E = x.shape
        H, D = (NUM_HEADS, HEAD_DIM)
        qkv = x @ w_qkv.T
        qkv = qkv.reshape(B, S, 3, H, D).transpose(2, 0, 3, 1, 4)
        q, k, v = (qkv[0], qkv[1], qkv[2])
        o = _sliding_window_attention(q, k, v)
        o = o.transpose(0, 2, 1, 3).reshape(B, S, E)
        return o @ w_out.T

    def _L1_ffn_ref(x, w_gate, w_up, w_down):
        import jax, jax.numpy as jnp
        import numpy as np
        DIM_IN = 256
        DIM_HIDDEN = 1024
        gate = jnp.einsum('bsd,hd->bsh', x, w_gate)
        up = jnp.einsum('bsd,hd->bsh', x, w_up)
        gated = jax.nn.silu(gate) * up
        return jnp.einsum('bsh,dh->bsd', gated, w_down)
    x = L0_attn_x
    x = _layernorm(x + _L0_attn_ref(x, L0_attn_A_log, L0_attn_D, L0_attn_x_proj_w, L0_attn_dt_proj_w, L0_attn_dt_proj_b), axis=-1)
    x = _layernorm(x + _L0_ffn_ref(x, L0_ffn_W_up, L0_ffn_W_gate, L0_ffn_W_down), axis=-1)
    x = _layernorm(x + _L1_attn_ref(x, L1_attn_w_qkv, L1_attn_w_out), axis=-1)
    x = _layernorm(x + _L1_ffn_ref(x, L1_ffn_w_gate, L1_ffn_w_up, L1_ffn_w_down), axis=-1)
    return x

_drawn_inputs = setup_inputs


def setup_inputs(seed=0):
    import zlib

    import numpy as np

    out = dict(_drawn_inputs(seed))
    spreads = {'L0_attn_D': (1.0, 0.6)}
    factors = {}
    for name, (base, spread) in spreads.items():
        noise = np.random.default_rng([zlib.crc32(name.encode()), seed]).standard_normal(out[name].shape)
        drawn = base * np.exp(spread * noise) if base else spread * noise
        out[name] = jnp.asarray(drawn.astype(out[name].dtype))
    for name, factor in factors.items():
        out[name] = (out[name] * factor).astype(out[name].dtype)
    return out
```

```python
import concourse.bass as bass
from concourse import mybir
from contextlib import ExitStack

F32 = mybir.dt.float32
F32R = mybir.dt.float32r
BF16 = mybir.dt.bfloat16
ALU = mybir.AluOpType
ACT = mybir.ActivationFunctionType
AX = mybir.AxisListType

P = 128
D = 256
DH = D // P
SEQ = 256
NSEQ = 2
T = NSEQ * SEQ
TT = T // P
NS = 16
E = 1024
EK = E // P
H = 16
HC = D // H
HG = 8
UNITS = NSEQ * DH
LN_EPS = 1e-5
Q_EPS = 1e-8
NEG = -1e30
SCALE = 1.0 / float(HC) ** 0.5
LAG = 3

REST = (
    [("turn_in",), ("norm", 0), ("turn", 0)]
    + [("ffn", 0, e) for e in range(EK)] + [("down", 0)] + [("norm", 1), ("turn", 1)]
    + [("qk",), ("v",)]
    + [(kind, u, b) for u in range(UNITS) for kind, b in
       [("score", b) for b in range(6)] + [("ptrans", b) for b in range(6)] + [("pv", 0)]]
    + [("out_proj",), ("norm", 2), ("turn", 2)]
    + [("ffn", 1, e) for e in range(EK)] + [("down", 1), ("norm", 3)]
)
WEIGHT = {"turn_in": 9, "norm": 25, "turn": 9, "qk": 68, "v": 35, "score": 11, "ptrans": 6, "pv": 20,
          "out_proj": 35}


def weight(piece):
    if piece[0] == "ffn":
        return 18 if piece[1] == 0 else 35
    if piece[0] == "down":
        return 70 if piece[1] == 0 else 138
    return WEIGHT[piece[0]]


def slots():
    total, at, out = sum(map(weight, REST)), 0, [[] for _ in range(NS)]
    for piece in REST:
        out[min(NS - 1, at * NS // total)].append(piece)
        at += weight(piece)
    return out


SLOTS = slots()


class Signal:

    def __init__(self, sem, per):
        self.sem, self.per = sem, per

    def wait(self, eng, step, count):
        if isinstance(step, int) and step < 0:
            return
        eng.wait_ge(self.sem, step * self.per + count)


def build(nc, xT, A_log, Dskip, xprojT, dtT, dt_b, wupT, wgateT, wdownT, wqkvT, woutT, wgT2, wuT2, wdT2, out):
    STEPS = xT.shape[1] // T
    with ExitStack() as ctx:
        def sb(name, shape, dt=F32):
            return ctx.enter_context(nc.sbuf_tensor(name, shape, dt))

        w_xp = sb("w_xp", [P, DH, 2 * P])
        w_dt = sb("w_dt", [P, D])
        w_qkv = sb("w_qkv", [P, DH, 3 * D])
        w_out = sb("w_out", [P, DH, D])
        w_up1 = sb("w_up1", [P, DH, E], F32R)
        w_gate1 = sb("w_gate1", [P, DH, E], F32R)
        w_down1 = sb("w_down1", [P, EK, D], F32R)
        w_gate2 = sb("w_gate2", [P, DH, E])
        w_up2 = sb("w_up2", [P, DH, E])
        w_down2 = sb("w_down2", [P, EK, D])
        ident = sb("ident", [P, P])
        ident_b = sb("ident_b", [P, P], BF16)
        pick = sb("pick", [P, 2 * NS], BF16)
        mask0 = sb("mask0", [P, P], BF16)
        mask1 = sb("mask1", [P, 192], BF16)
        ones = sb("ones", [P, P])
        half_neg = sb("half_neg", [P, TT])
        A_neg = sb("A_neg", [P, DH, NS])
        d_one = sb("d_one", [P, DH])
        b_dt = sb("b_dt", [P, DH])
        q_sum = sb("q_sum", [P, 4])
        q_thr = sb("q_thr", [P, 8])
        x_ch = sb("x_ch", [P, DH, T])
        dr = sb("dr", [P, T])
        delta = sb("delta", [P, DH, T])
        du = sb("du", [P, DH, T])
        bc_parts = sb("bc_parts", [P, T], BF16)
        bc_rest = sb("bc_rest", [P, T])
        bc_mid = sb("bc_mid", [P, T], BF16)
        dA = sb("dA", [P, 2, DH, T])
        hs = sb("hs", [P, 4, DH, T])
        cs = sb("cs", [P, 2, T])
        r_ch = sb("r_ch", [P, DH, T])
        x_tok = sb("x_tok", [P, TT, D])
        pause = sb("pause", [P, 1])
        stats = sb("stats", [P, TT, 6])
        mv = sb("mv", [P, TT, 2])
        var_eps = sb("var_eps", [P, TT])
        rstd = sb("rstd", [P, TT])
        x_hi = sb("x_hi", [P, DH, T], F32R)
        x_lo = sb("x_lo", [P, DH, T], F32R)
        th = sb("th", [P, 2, T])
        mm = sb("mm", [P, 2, T])
        hid = sb("hid", [P, 2, T])
        Kx = sb("Kx", [P, 2, HG, SEQ])
        Vz = sb("Vz", [P, TT, H, 2 * HC])
        nb = sb("nb", [P, 2, 2, 16])
        den = sb("den", [P, 2, 16])
        rden = sb("rden", [P, 16])
        rden_x = sb("rden_x", [P, 16, HC])
        P0 = sb("P0", [P, HG, P])
        P1 = sb("P1", [P, HG, SEQ])
        region = nc.sbuf_base
        h_hi = sb("h_hi", [P, EK, T], F32R)
        h_lo = sb("h_lo", [P, EK, T], F32R)

        def over(name, shape, at, dt=F32):
            return nc.alloc_sbuf_tensor_at(name, shape, dt, offset=region + at)

        KB = 1024
        w_raw = over("w_raw", [P, 3, 2 * E], 0)
        h2 = over("h2", [P, EK, T], 0)
        q_ch = over("q_ch", [P, DH, T], 0)
        k_ch = over("k_ch", [P, DH, T], 4 * KB)
        PT0 = over("PT0", [P, HG, SEQ], 8 * KB)
        PT1 = over("PT1", [P, HG, P], 16 * KB)
        o_ch = over("o_ch", [P, DH, T], 20 * KB)
        rd_ch = over("rd_ch", [P, SEQ], 24 * KB)
        x_t = over("x_t", [P, DH, T], 26 * KB)
        w_abs = hs

        ps = [ctx.enter_context(nc.psum_tensor(f"ps{i}", [P, 512], F32)) for i in range(8)]
        bankB, bankC, Y, W = ps[0], ps[1], ps[2:4], ps[4:8]

        def sem(name):
            return ctx.enter_context(nc.semaphore(name))

        def sig(name, per):
            return Signal(sem(name), per)

        s_load = [sem(f"loaded_{n}") for n in range(4)]
        s_const = sem("const_made")
        s_prep = sem("prep_vector")
        s_preps = sem("prep_scalar")
        s_prept = sem("prep_tensor")
        x_in = sig("x_loaded", 16)
        xdbl = sig("xdbl_made", 2)
        drc = sig("dr_copied", 1)
        bch = sig("bc_high", 1)
        bcs = sig("bc_split", 4)
        dtp = sig("dt_made", 2)
        sp = sig("softplus_steps", 6)
        dl = sig("delta_steps", 6)
        bb = sig("B_spread", NS)
        bc = sig("C_spread", NS)
        exa = sig("dA_made", NS)
        ccp = sig("C_copied", NS)
        dbu = sig("dBu_made", NS)
        scn = sig("scanned", NS)
        hc = sig("hC_made", NS)
        red = sig("summed", NS)
        rt = sig("r_made", 2)
        tra = sig("r_turned", 1)
        rr = sig("residual_added", 6)
        st = sig("stats_steps", 12)
        pw = sig("rstd_made", 4)
        xn = sig("normed", 4)
        trx = sig("x_turned", 6)
        xh = sig("x_high", 2)
        xl = sig("x_low", 2)
        xe = sig("x_copied", 4)
        ug = sig("up_gate_made", 32)
        thd = sig("tanh_made", 16)
        mmd = sig("silu_made", 16)
        hd = sig("hidden_made", 16)
        hh = sig("hidden_high", 8)
        hl = sig("hidden_low", 8)
        dn = sig("projected", 6)
        qk = sig("qk_made", 4)
        qa = sig("qk_copied_scalar", 2)
        qd = sig("qk_copied_vector", 2)
        vp = sig("v_made", 2)
        vz = sig("v_copied", 4)
        kx = [sig(f"k_spread_{u}", 16 * HG) for u in range(UNITS)]
        sc = sig("scores_made", 6 * UNITS)
        nbs = sig("max_steps", 12 * UNITS)
        ex = sig("exps_made", 6 * UNITS)
        rds = sig("rden_made", 2 * UNITS)
        tt = sig("probs_turned", 6 * UNITS)
        ptd = sig("pt_copied_vector", 3 * UNITS)
        pta = sig("pt_copied_scalar", 3 * UNITS)
        rdt = sig("rden_turned", UNITS)
        rdc = sig("rden_copied", UNITS)
        pv = sig("pv_made", UNITS)
        ot = sig("o_made", UNITS)
        odma = sig("stored", 16)

        def ring(r):
            return W[r % 3]

        def steps(eng, fill, scan_step, tail, rest):
            def step(i, j):
                if i is not None:
                    fill(i)
                for n in range(NS):
                    if i is not None:
                        scan_step(i, n)
                    if j is not None:
                        for piece in SLOTS[n]:
                            rest(j, *piece)
                if i is not None:
                    tail(i)

            step(0, None)
            step(1, 0)
            with eng.Fori(2, STEPS) as i:
                step(i, i - 1)
            step(None, STEPS - 1)

        block = ctx.enter_context(nc.Block())

        @block.sync
        def _(sp_):
            def load(dst, src, lot):
                sp_.dma_start(dst, src).then_inc(s_load[lot], 16)

            load(w_xp[:], xprojT.rearrange("(k p) e -> p k e", p=P), 0)
            sp_.dma_start(x_ch[:], xT[:, 0:T].rearrange("(k p) t -> p k t", p=P)).then_inc(x_in.sem, 16)
            load(w_dt[:], dtT, 0)
            load(A_neg[:], A_log.rearrange("(k p) n -> p k n", p=P), 2)
            load(d_one[:], Dskip, 2)
            load(b_dt[:], dt_b, 2)
            for n, (w, rows) in enumerate(((wupT, DH), (wgateT, DH), (wdownT, EK))):
                load(w_raw[:, n, :].rearrange("p (k e) -> p k e", k=rows),
                     w.rearrange("(k p) e -> p k e", p=P), 1)
            for dst, w in ((w_qkv, wqkvT), (w_out, woutT), (w_gate2, wgT2), (w_up2, wuT2), (w_down2, wdT2)):
                load(dst[:], w.rearrange("(k p) e -> p k e", p=P), 3)

            def fill(i):
                pass

            def scan_step(i, n):
                pass

            def tail(i, at):
                rt.wait(sp_, i, 2)
                sp_.dma_start(x_ch[:], xT_next[:, at].rearrange("(k p) t -> p k t", p=P)
                              ).then_inc(x_in.sem, 16)

            def rest(j, at_out, kind, *at):
                if kind == "score" and at[1] == 0:
                    u = at[0]
                    s, g = u // DH, u % DH
                    if u < 2:
                        (qa if g == 0 else qd).wait(sp_, j, 2)
                    else:
                        sc.wait(sp_, j, (u - 1) * 6)
                    for h in range(HG):
                        rows = slice(h * HC, (h + 1) * HC)
                        sp_.dma_start(Kx[rows, u % 2, h, :], k_ch[rows, g, s * SEQ:(s + 1) * SEQ]
                                      ).then_inc(kx[u].sem, 16)
                if kind == "norm" and at[0] == 3:
                    xn.wait(sp_, j, 4)
                    sp_.dma_start(out[at_out, :].rearrange("(t p) d -> p t d", p=P),
                                  x_tok[:]).then_inc(odma.sem, 16)

            xT_next = xT[:, T:]

            def one(i, j):
                if isinstance(j, int):
                    at_out, at_x = slice(j * T, (j + 1) * T), slice((j + 1) * T, (j + 2) * T)
                else:
                    at_out, at_x = bass.ds(sp_.snap(j * T), T), bass.ds(sp_.snap(i * T), T)
                for n in range(NS):
                    for piece in SLOTS[n]:
                        rest(j, at_out, *piece)
                if i is not None:
                    tail(i, at_x)

            tail(0, slice(0, T))
            one(1, 0)
            with sp_.Fori(2, STEPS - 1) as i:
                one(i, i - 1)
            one(None, STEPS - 2)
            one(None, STEPS - 1)
            odma.wait(sp_, STEPS - 1, 16)

        @block.gpsimd
        def _(pool):
            pool.memset(ident[:], 0.0).then_inc(s_const, 1)
            pool.memset(ident_b[:], 0.0).then_inc(s_const, 1)
            pool.memset(pick[:], 0.0).then_inc(s_const, 1)
            pool.memset(mask0[:], 0.0).then_inc(s_const, 1)
            pool.memset(mask1[:], 0.0).then_inc(s_const, 1)
            pool.memset(ones[:], 1.0).then_inc(s_const, 1)
            pool.memset(half_neg[:], -0.5).then_inc(s_const, 1)
            pool.wait_ge(s_const, 7)
            pool.affine_select(out=ident[:], in_=ident[:], compare_op=ALU.not_equal, fill=1.0, base=0,
                               pattern=[[-1, P]], channel_multiplier=1).then_inc(s_const, 1)
            pool.affine_select(out=ident_b[:], in_=ident_b[:], compare_op=ALU.not_equal, fill=1.0, base=0,
                               pattern=[[-1, P]], channel_multiplier=1).then_inc(s_const, 1)
            for c in range(3):
                pool.affine_select(out=pick[:], in_=pick[:], compare_op=ALU.not_equal, fill=1.0, base=-32 * c,
                                   pattern=[[-1, 2 * NS]], channel_multiplier=1).then_inc(s_const, 1)
                pool.wait_ge(s_const, 10 + c)
            for m, w, lo in ((mask0, P, 0), (mask1, 192, 64)):
                pool.affine_select(out=m[:], in_=m[:], compare_op=ALU.is_ge, fill=NEG, base=lo,
                                   pattern=[[-1, w]], channel_multiplier=1).then_inc(s_const, 1)
            pool.wait_ge(s_const, 14)
            for m, w, lo in ((mask0, P, 0), (mask1, 192, 64)):
                pool.affine_select(out=m[:], in_=m[:], compare_op=ALU.is_ge, fill=NEG, base=64 - lo,
                                   pattern=[[1, w]], channel_multiplier=-1).then_inc(s_const, 1)
            for n in range(2):
                for s in range(NSEQ):
                    pool.memset(dA[:, n, :, s * SEQ:s * SEQ + 1], 0.0).then_inc(s_const, 1)
            pool.memset(Kx[:], 0.0).then_inc(s_const, 1)
            pool.memset(Vz[:], 0.0).then_inc(s_const, 1)
            pool.memset(P1[:, :, 0:64], 0.0).then_inc(s_const, 1)

            def fill(i):
                pass

            def scan_step(i, n):
                scn.wait(pool, i, n + 1)
                ccp.wait(pool, i, n + 1)
                pool.tensor_tensor(hs[:, n % 4], hs[:, n % 4],
                                   cs[:, n % 2].unsqueeze(1).broadcast_to([P, DH, T]), ALU.mult
                                   ).then_inc(hc.sem, 1)

            def rest(j, kind, *at):
                if kind == "norm":
                    st.wait(pool, j, 3 * at[0] + 3)
                    pool.tensor_tensor(rstd[:], var_eps[:], half_neg[:], ALU.pow).then_inc(pw.sem, 1)
                elif kind == "ffn" and at[0] == 0:
                    e = at[1]
                    hh.wait(pool, j, e + 1)
                    pool.tensor_tensor(h_lo[:, e], hid[:, e % 2], h_hi[:, e].bitcast(F32), ALU.subtract
                                       ).then_inc(hl.sem, 1)

            steps(pool, fill, scan_step, fill, rest)

        @block.scalar
        def _(act):
            act.wait_ge(s_load[2], 48)
            act.activation(A_neg[:], A_neg[:], ACT.Exp).then_inc(s_preps, 1)
            act.wait_ge(s_load[1], 48)
            for n in range(3):
                act.activation(w_abs[:, 0:2].rearrange("p n a b -> p (n a b)"), w_raw[:, n], ACT.Abs,
                               accum_out=q_sum[:, n:n + 1]).then_inc(s_preps, 1)
                act.wait_ge(s_preps, 2 + n)
            act.wait_ge(s_const, 23)
            act.wait_ge(s_prep, 9)

            def fill(i):
                xdbl.wait(act, i, 1)
                act.activation(dr[:], bankB[:], ACT.Copy).then_inc(drc.sem, 1)
                xdbl.wait(act, i, 2)
                act.activation(bc_parts[:], bankC[:], ACT.Copy).then_inc(bch.sem, 1)
                for h in range(DH):
                    dtp.wait(act, i, h + 1)
                    act.activation(delta[:, h], (bankB, bankC)[h][:], ACT.Abs, bias=b_dt[:, h:h + 1]
                                   ).then_inc(sp.sem, 1)
                for h in range(DH):
                    sp.wait(act, i, 1 + h)
                    act.activation(delta[:, h], delta[:, h], ACT.Exp, scale=-1.0).then_inc(sp.sem, 1)
                for h in range(DH):
                    sp.wait(act, i, 3 + h)
                    act.activation(delta[:, h], delta[:, h], ACT.Ln, bias=1.0).then_inc(sp.sem, 1)

            def scan_step(i, n):
                if n == 0:
                    dl.wait(act, i, 4)
                if n >= 2:
                    scn.wait(act, i, n - 1)
                else:
                    scn.wait(act, i - 1, 15 + n)
                for h in range(DH):
                    last = act.activation(
                        dA[:, n % 2, h].rearrange("p (s t) -> p s t", s=NSEQ)[:, :, 1:],
                        delta[:, h].rearrange("p (s t) -> p s t", s=NSEQ)[:, :, 1:],
                        ACT.Exp, scale=A_neg[:, h, n:n + 1])
                last.then_inc(exa.sem, 1)
                bc.wait(act, i, n + 1)
                if n >= 2:
                    hc.wait(act, i, n - 1)
                else:
                    hc.wait(act, i - 1, 15 + n)
                act.activation(cs[:, n % 2], bankC[:], ACT.Copy).then_inc(ccp.sem, 1)

            def tail(i):
                pass

            def high(j, e):
                hd.wait(act, j, e + 1)
                act.activation(h_hi[:, e], hid[:, e % 2], ACT.Copy).then_inc(hh.sem, 1)

            def rest(j, kind, *at):
                if kind == "turn":
                    k = at[0]
                    for c in range(DH):
                        trx.wait(act, j, 2 * k + c + 1)
                        if k == 0:
                            act.activation(x_hi[:, c], W[2 + c][:], ACT.Copy).then_inc(xh.sem, 1)
                        else:
                            act.activation(x_t[:, c], W[2 + c][:], ACT.Copy).then_inc(xe.sem, 1)
                elif kind == "ffn":
                    f, e = at
                    ug.wait(act, j, 16 * f + 2 * e + 1)
                    if e >= 2:
                        hd.wait(act, j, 8 * f + e - 1)
                    act.activation(th[:, e % 2], W[2 * (e % 2)][:], ACT.Tanh,
                                   scale=q_thr[:, 6:7] if f == 0 else 0.5).then_inc(thd.sem, 1)
                    if f == 0 and e >= 1:
                        high(j, e - 1)
                elif kind == "down" and at[0] == 0:
                    high(j, EK - 1)
                elif kind == "qk":
                    for m in (0, 2):
                        qk.wait(act, j, m + 1)
                        act.activation((q_ch if m == 0 else k_ch)[:, 0], W[m][:], ACT.Copy).then_inc(qa.sem, 1)
                elif kind == "score":
                    u, b = at
                    nbs.wait(act, j, 12 * u + 2 * b + 2)
                    if b == 0 and u > 0:
                        tt.wait(act, j, 6 * u)
                    heads = range(4 * b, 4 * b + 4) if b < 2 else range(2 * (b - 2), 2 * (b - 2) + 2)
                    wid = P if b < 2 else 192
                    for n, h in enumerate(heads):
                        dst = P0[:, h] if b < 2 else P1[:, h, 64:SEQ]
                        col = h if b < 2 else HG + h
                        last = act.activation(dst, ring(12 * u + b)[:, n * wid:(n + 1) * wid], ACT.Exp,
                                              scale=SCALE, bias=nb[:, u % 2, 1, col:col + 1],
                                              accum_out=den[:, u % 2, col:col + 1])
                    last.then_inc(ex.sem, 1)
                elif kind == "ptrans":
                    u, b = at
                    if b % 2:
                        tt.wait(act, j, 6 * u + b + 1)
                        if u > 0 and b == 1:
                            pv.wait(act, j, u)
                        dst = PT0[:, 2 * b:2 * b + 2] if b < 4 else PT1[:, 4 * (b - 4):4 * (b - 4) + 4]
                        act.activation(dst.rearrange("p a b -> p (a b)"), ring(12 * u + 6 + b)[:], ACT.Copy
                                       ).then_inc(pta.sem, 1)
                elif kind == "pv":
                    u = at[0]
                    rdt.wait(act, j, u + 1)
                    if u > 0:
                        ot.wait(act, j, u)
                    act.activation(rd_ch[:], W[3][:, SEQ:2 * SEQ], ACT.Copy).then_inc(rdc.sem, 1)

            steps(act, fill, scan_step, tail, rest)

        @block.vector
        def _(dve):
            dve.wait_ge(s_preps, 1)
            dve.tensor_scalar(A_neg[:], A_neg[:], -1.0, None, ALU.mult).then_inc(s_prep, 1)
            dve.tensor_scalar(d_one[:], d_one[:], 1.0, None, ALU.add).then_inc(s_prep, 1)
            dve.wait_ge(s_prept, 1)
            dve.tensor_scalar(q_sum[:, 0:3], W[0][:, 0:3], 1.0 / (D * E), Q_EPS, ALU.mult, ALU.add
                              ).then_inc(s_prep, 1)
            dve.wait_ge(s_prep, 3)
            dve.tensor_scalar(q_thr[:, 0:3], q_sum[:, 0:3], 0.5, None, ALU.mult).then_inc(s_prep, 1)
            dve.tensor_scalar(q_thr[:, 3:6], q_sum[:, 0:3], -0.5, None, ALU.mult).then_inc(s_prep, 1)
            dve.wait_ge(s_prep, 5)
            dve.tensor_scalar(q_thr[:, 6:7], q_thr[:, 0:1], 1.0, None, ALU.mult).then_inc(s_prep, 1)
            dve.tensor_tensor(q_thr[:, 7:8], q_thr[:, 0:1], q_sum[:, 1:2], ALU.mult).then_inc(s_prep, 1)
            dve.wait_ge(s_prep, 7)
            dve.tensor_tensor(q_thr[:, 7:8], q_thr[:, 7:8], q_sum[:, 2:3], ALU.mult).then_inc(s_prep, 1)
            for n, w in enumerate((w_up1, w_gate1, w_down1)):
                low = w_abs[:, 0:2].rearrange("p n a b -> p (n a b)")
                dve.wait_ge(s_preps, 4)
                if n:
                    dve.wait_ge(s_prep, 9 + 2 * n - 1)
                dve.tensor_scalar(low, w_raw[:, n], q_thr[:, 3 + n:4 + n], None, ALU.is_lt).then_inc(s_prep, 1)
                dve.wait_ge(s_prep, 9 + 2 * n)
                dve.scalar_tensor_tensor(w[:].rearrange("p k e -> p (k e)"), w_raw[:, n], q_thr[:, n:n + 1],
                                         low, ALU.is_gt, ALU.subtract).then_inc(s_prep, 1)
            dve.wait_ge(s_prep, 14)
            dve.wait_ge(s_const, 23)

            def fill(i):
                bch.wait(dve, i, 1)
                dve.tensor_tensor(bc_rest[:], bankC[:], bc_parts[:], ALU.subtract).then_inc(bcs.sem, 1)
                bcs.wait(dve, i, 1)
                dve.tensor_copy(bc_parts[32:64], bc_rest[32:64]).then_inc(bcs.sem, 1)
                dve.tensor_copy(bc_mid[64:96], bc_rest[64:96]).then_inc(bcs.sem, 1)
                bcs.wait(dve, i, 3)
                dve.tensor_tensor(bc_parts[64:96], bc_rest[64:96], bc_mid[64:96], ALU.subtract
                                  ).then_inc(bcs.sem, 1)
                for h in range(DH):
                    sp.wait(dve, i, h + 1)
                    dve.tensor_scalar(du[:, h], (bankB, bankC)[h][:], b_dt[:, h:h + 1], 0.0, ALU.add, ALU.max
                                      ).then_inc(dl.sem, 1)
                for h in range(DH):
                    sp.wait(dve, i, 5 + h)
                    dl.wait(dve, i, 1 + h)
                    dve.tensor_tensor(delta[:, h], du[:, h], delta[:, h], ALU.add).then_inc(dl.sem, 1)
                x_in.wait(dve, i, 16)
                for h in range(DH):
                    dl.wait(dve, i, 3 + h)
                    dve.tensor_tensor(du[:, h], delta[:, h], x_ch[:, h], ALU.mult).then_inc(dl.sem, 1)

            def scan_step(i, n):
                if n == 0:
                    dl.wait(dve, i, 6)
                bb.wait(dve, i, n + 1)
                if n >= 4:
                    red.wait(dve, i, n - 3)
                else:
                    red.wait(dve, i - 1, 13 + n)
                dve.tensor_tensor(hs[:, n % 4], du[:], bankB[:].unsqueeze(1).broadcast_to([P, DH, T]), ALU.mult
                                  ).then_inc(dbu.sem, 1)
                dbu.wait(dve, i, n + 1)
                exa.wait(dve, i, n + 1)
                flat = hs[:, n % 4].rearrange("p h t -> p (h t)")
                dve.tensor_tensor_scan(flat, dA[:, n % 2].rearrange("p h t -> p (h t)"), flat, 0.0,
                                       ALU.mult, ALU.add).then_inc(scn.sem, 1)

            def tail(i):
                red.wait(dve, i, NS)
                tra.wait(dve, i - 1, 1)
                for h in range(DH):
                    dve.scalar_tensor_tensor(r_ch[:, h], x_ch[:, h], d_one[:, h:h + 1], Y[h][:], ALU.mult, ALU.add
                                             ).then_inc(rt.sem, 1)

            def rest(j, kind, *at):
                if kind == "norm":
                    k = at[0]
                    if k == 0:
                        tra.wait(dve, j, 1)
                        odma.wait(dve, j - 1, 16)
                        src = [W[t // 2][:, (t % 2) * D:(t % 2 + 1) * D] for t in range(TT)]
                    else:
                        scale = (q_thr[:, 7:8], 1.0, 0.5)[k - 1]
                        for c in range(2):
                            dn.wait(dve, j, 2 * k - 1 + c)
                            x2 = x_tok[:, 2 * c:2 * c + 2].rearrange("p a b -> p (a b)")
                            dve.scalar_tensor_tensor(x2, W[c][:], scale, x2, ALU.mult, ALU.add
                                                     ).then_inc(rr.sem, 1)
                        rr.wait(dve, j, 2 * k)
                        src = [x_tok[:, t] for t in range(TT)]
                    for t in range(TT):
                        last = dve.bn_stats(stats[:, t], src[t])
                    last.then_inc(st.sem, 1)
                    st.wait(dve, j, 3 * k + 1)
                    dve.memset(pause[:], 0.0)
                    for t in range(TT):
                        last = dve.bn_aggr(mv[:, t], stats[:, t])
                    last.then_inc(st.sem, 1)
                    st.wait(dve, j, 3 * k + 2)
                    dve.tensor_scalar(var_eps[:], mv[:, :, 1], LN_EPS, None, ALU.add).then_inc(st.sem, 1)
                    pw.wait(dve, j, k + 1)
                    for t in range(TT):
                        last = dve.tensor_scalar(x_tok[:, t], src[t], mv[:, t, 0:1], rstd[:, t:t + 1],
                                                 ALU.subtract, ALU.mult)
                    last.then_inc(xn.sem, 1)
                elif kind == "turn" and at[0] == 0:
                    for c in range(DH):
                        xh.wait(dve, j, c + 1)
                        dve.tensor_tensor(x_lo[:, c], W[2 + c][:], x_hi[:, c].bitcast(F32), ALU.subtract
                                          ).then_inc(xl.sem, 1)
                elif kind == "ffn":
                    f, e = at
                    thd.wait(dve, j, 8 * f + e + 1)
                    dve.scalar_tensor_tensor(mm[:, e % 2], th[:, e % 2], 1.0, W[2 * (e % 2)][:],
                                             ALU.add, ALU.mult).then_inc(mmd.sem, 1)
                    mmd.wait(dve, j, 8 * f + e + 1)
                    ug.wait(dve, j, 16 * f + 2 * e + 2)
                    if f == 0 and e >= 2:
                        hl.wait(dve, j, e - 1)
                    dve.tensor_tensor(hid[:, e % 2] if f == 0 else h2[:, e], mm[:, e % 2],
                                      W[2 * (e % 2) + 1][:], ALU.mult).then_inc(hd.sem, 1)
                elif kind == "qk":
                    for m in (1, 3):
                        qk.wait(dve, j, m + 1)
                        dve.tensor_copy((q_ch if m == 1 else k_ch)[:, 1], W[m][:]).then_inc(qd.sem, 1)
                elif kind == "v":
                    for c in range(2):
                        vp.wait(dve, j, c + 1)
                        for odd in range(2):
                            dst = Vz[:, 2 * c:2 * c + 2].rearrange("p t (a o) d -> p t a o d", o=2)
                            src = W[c][:].rearrange("p (t a o d) -> p t a o d", t=2, a=HG, o=2)
                            dve.tensor_copy(dst[:, :, :, odd, HC * odd:HC * odd + HC], src[:, :, :, odd, :]
                                            ).then_inc(vz.sem, 1)
                elif kind == "score":
                    u, b = at
                    sc.wait(dve, j, 6 * u + b + 1)
                    n, wid = (4, P) if b < 2 else (2, 192)
                    col = 4 * b if b < 2 else HG + 2 * (b - 2)
                    dve.tensor_reduce(nb[:, u % 2, 0, col:col + n],
                                      ring(12 * u + b)[:, :n * wid].rearrange("p (n w) -> p n w", n=n),
                                      AX.X, ALU.max).then_inc(nbs.sem, 1)
                    nbs.wait(dve, j, 12 * u + 2 * b + 1)
                    dve.tensor_scalar(nb[:, u % 2, 1, col:col + n], nb[:, u % 2, 0, col:col + n], -SCALE, None,
                                      ALU.mult).then_inc(nbs.sem, 1)
                elif kind == "ptrans":
                    u, b = at
                    if b % 2 == 0:
                        tt.wait(dve, j, 6 * u + b + 1)
                        if u > 0 and b == 0:
                            pv.wait(dve, j, u)
                        dst = PT0[:, 2 * b:2 * b + 2] if b < 4 else PT1[:, 4 * (b - 4):4 * (b - 4) + 4]
                        dve.tensor_copy(dst.rearrange("p a b -> p (a b)"), ring(12 * u + 6 + b)[:]
                                        ).then_inc(ptd.sem, 1)
                    if b == 0:
                        ex.wait(dve, j, 6 * u + 6)
                        dve.reciprocal(rden[:], den[:, u % 2]).then_inc(rds.sem, 1)
                        rds.wait(dve, j, 2 * u + 1)
                        if u:
                            rdt.wait(dve, j, u)
                        dve.tensor_copy(rden_x[:], rden[:].unsqueeze(2).broadcast_to([P, 16, HC])
                                        ).then_inc(rds.sem, 1)
                elif kind == "pv":
                    u = at[0]
                    s, g = u // DH, u % DH
                    rdc.wait(dve, j, u + 1)
                    pv.wait(dve, j, u + 1)
                    dve.tensor_tensor(o_ch[:, g, s * SEQ:(s + 1) * SEQ], W[3][:, 0:SEQ], rd_ch[:], ALU.mult
                                      ).then_inc(ot.sem, 1)

            steps(dve, fill, scan_step, tail, rest)

        @block.tensor
        def _(pe):
            pe.wait_ge(s_preps, 4)
            pe.wait_ge(s_const, 7)
            nc.tensor.matmul(W[0][:, 0:3], ones[:], q_sum[:, 0:3], start=True, stop=True).then_inc(s_prept, 1)
            pe.wait_ge(s_load[0], 32)
            pe.wait_ge(s_const, 23)
            pe.wait_ge(s_prep, 14)

            def acc(dst, pairs):
                for n, (l, r) in enumerate(pairs):
                    last = nc.tensor.matmul(dst, l, r, start=n == 0, stop=n == len(pairs) - 1)
                return last

            def fill(i):
                x_in.wait(pe, i, 16)
                dbu.wait(pe, i - 1, NS)
                ccp.wait(pe, i - 1, NS)
                for m, bank in enumerate((bankB, bankC)):
                    acc(bank[:], [(w_xp[:, k, m * P:(m + 1) * P], x_ch[:, k]) for k in range(DH)]
                        ).then_inc(xdbl.sem, 1)
                drc.wait(pe, i, 1)
                acc(bankB[:], [(w_dt[:, 0:P], dr[:])]).then_inc(dtp.sem, 1)
                bcs.wait(pe, i, 1)
                acc(bankC[:], [(w_dt[:, P:D], dr[:])]).then_inc(dtp.sem, 1)

            def add(i, n):
                hc.wait(pe, i, n + 1)
                if n == 0:
                    rt.wait(pe, i - 1, 2)
                for h in range(DH):
                    last = nc.tensor.matmul(Y[h][:], ident[:], hs[:, n % 4, h], start=n == 0, stop=n == NS - 1)
                last.then_inc(red.sem, 1)

            def scan_step(i, n):
                if n == 0:
                    bcs.wait(pe, i, 4)
                    dl.wait(pe, i, 2)
                    sp.wait(pe, i, 2)
                else:
                    dbu.wait(pe, i, n)
                nc.tensor.matmul(bankB[:], pick[:, n:n + 1].broadcast_to([P, P]), bc_parts[:],
                                 start=True, stop=True).then_inc(bb.sem, 1)
                if n:
                    ccp.wait(pe, i, n)
                nc.tensor.matmul(bankC[:], pick[:, NS + n:NS + n + 1].broadcast_to([P, P]), bc_parts[:],
                                 start=True, stop=True).then_inc(bc.sem, 1)
                if n >= LAG:
                    add(i, n - LAG)

            def tail(i):
                for n in range(NS - LAG, NS):
                    add(i, n)

            def ring_free(j, r):
                u, b = divmod(r - 3, 12)
                if r < 3:
                    vz.wait(pe, j, (2, 4, 4)[r])
                    return
                if b < 6:
                    ex.wait(pe, j, 6 * u + b + 1)
                elif b % 2 == 0:
                    ptd.wait(pe, j, 3 * u + (b - 6) // 2 + 1)
                else:
                    pta.wait(pe, j, 3 * u + (b - 6) // 2 + 1)

            def rest(j, kind, *at):
                if kind == "turn_in":
                    rt.wait(pe, j, 2)
                    rr.wait(pe, j - 1, 6)
                    for t in range(TT):
                        for c in range(DH):
                            last = nc.tensor.transpose(W[t // 2][:, (t % 2) * D + c * P:(t % 2) * D + (c + 1) * P],
                                                       r_ch[:, c, t * P:(t + 1) * P], ident[:])
                    last.then_inc(tra.sem, 1)
                elif kind == "turn":
                    xn.wait(pe, j, at[0] + 1)
                    if at[0] == 2:
                        ot.wait(pe, j, UNITS)
                    for c in range(DH):
                        for t in range(TT):
                            last = nc.tensor.transpose(W[2 + c][:, t * P:(t + 1) * P],
                                                       x_tok[:, t, c * P:(c + 1) * P], ident[:])
                        last.then_inc(trx.sem, 1)
                elif kind == "ffn":
                    f, e = at
                    if e == 0:
                        (xl if f == 0 else xe).wait(pe, j, 2 if f == 0 else 4)
                    if e >= 2:
                        hd.wait(pe, j, 8 * f + e - 1)
                    for n in range(2):
                        cols = slice(e * P, (e + 1) * P)
                        if f == 0:
                            w = (w_up1, w_gate1)[n]
                            pairs = [(w[:, k, cols], x[:, k]) for k in range(DH) for x in (x_lo, x_hi)]
                        else:
                            w = (w_gate2, w_up2)[n]
                            pairs = [(w[:, k, cols], x_t[:, k]) for k in range(DH)]
                        acc(W[2 * (e % 2) + n][:], pairs).then_inc(ug.sem, 1)
                elif kind == "down":
                    f = at[0]
                    hd.wait(pe, j, 8 * f + 8)
                    if f == 0:
                        hl.wait(pe, j, EK)
                    for t in range(TT):
                        rows = slice(t * P, (t + 1) * P)
                        if f == 0:
                            pairs = [(x[:, e, rows], w_down1[:, e]) for e in range(EK) for x in (h_lo, h_hi)]
                        else:
                            pairs = [(h2[:, e, rows], w_down2[:, e]) for e in range(EK)]
                        last = acc(W[t // 2][:, (t % 2) * D:(t % 2 + 1) * D], pairs)
                        if t % 2:
                            last.then_inc(dn.sem, 1)
                elif kind == "qk":
                    xe.wait(pe, j, 2)
                    for m in range(4):
                        acc(W[m][:], [(w_qkv[:, k, m * P:(m + 1) * P], x_t[:, k]) for k in range(DH)]
                            ).then_inc(qk.sem, 1)
                elif kind == "v":
                    qa.wait(pe, j, 1)
                    qd.wait(pe, j, 1)
                    for t in range(TT):
                        last = acc(W[t // 2][:, (t % 2) * D:(t % 2 + 1) * D],
                                   [(x_t[:, k, t * P:(t + 1) * P], w_qkv[:, k, 2 * D:3 * D]) for k in range(DH)])
                        if t % 2:
                            last.then_inc(vp.sem, 1)
                elif kind == "score":
                    u, b = at
                    s, g = u // DH, u % DH
                    if b == 0:
                        kx[u].wait(pe, j, 16 * HG)
                        qa.wait(pe, j, 2)
                        qd.wait(pe, j, 2)
                    ring_free(j, 12 * u + b)
                    q0 = s * SEQ + (0 if b < 2 else P)
                    if b < 2:
                        k_, m_, n, wid = Kx[:, u % 2, 4 * b:4 * b + 4, 0:P], mask0, 4, P
                    else:
                        k_, m_, n, wid = Kx[:, u % 2, 2 * (b - 2):2 * (b - 2) + 2, 64:SEQ], mask1, 2, 192
                    dst = ring(12 * u + b)[:, :n * wid].rearrange("p (n w) -> p n w", n=n)
                    nc.tensor.matmul(dst, q_ch[:, g, q0:q0 + P], k_, start=True, stop=False)
                    nc.tensor.matmul(dst, ident_b[:], m_[:].unsqueeze(1).broadcast_to([P, n, wid]),
                                     start=False, stop=True).then_inc(sc.sem, 1)
                elif kind == "ptrans":
                    u, b = at
                    ex.wait(pe, j, 6 * u + (3, 4, 5, 6, 6, 6)[b])
                    ring_free(j, 12 * u + 6 + b)
                    if b < 4:
                        src = [x for h in (2 * b, 2 * b + 1) for x in (P0[:, h], P1[:, h, 0:P])]
                    else:
                        src = [P1[:, h, P:SEQ] for h in range(4 * (b - 4), 4 * (b - 4) + 4)]
                    for n, x in enumerate(src):
                        last = nc.tensor.transpose(ring(12 * u + 6 + b)[:, n * P:(n + 1) * P], x, ident[:])
                    last.then_inc(tt.sem, 1)
                elif kind == "pv":
                    u = at[0]
                    s, g = u // DH, u % DH
                    rds.wait(pe, j, 2 * u + 2)
                    if u:
                        ot.wait(pe, j, u)
                    for q in range(2):
                        src = rden_x[:, q * HG:(q + 1) * HG].rearrange("p h c -> p (h c)")
                        last = nc.tensor.transpose(W[3][:, SEQ + q * P:SEQ + (q + 1) * P], src, ident[:])
                    last.then_inc(rdt.sem, 1)
                    ptd.wait(pe, j, 3 * u + 3)
                    pta.wait(pe, j, 3 * u + 3)
                    vz.wait(pe, j, 4)
                    rdc.wait(pe, j, u + 1)
                    for pr in range(HG // 2):
                        rows = slice(32 * pr, 32 * pr + 32)
                        for n, h in enumerate((2 * pr, 2 * pr + 1)):
                            last = nc.tensor.matmul(W[3][rows, 0:SEQ], Vz[:, 2 * s, g * HG + h], PT0[:, h],
                                                    start=n == 0, stop=False)
                            last = nc.tensor.matmul(W[3][rows, P:SEQ], Vz[:, 2 * s + 1, g * HG + h], PT1[:, h],
                                                    start=False, stop=n == 1)
                    last.then_inc(pv.sem, 1)
                elif kind == "out_proj":
                    ot.wait(pe, j, UNITS)
                    for t in range(TT):
                        last = acc(W[t // 2][:, (t % 2) * D:(t % 2 + 1) * D],
                                   [(o_ch[:, k, t * P:(t + 1) * P], w_out[:, k]) for k in range(DH)])
                        if t % 2:
                            last.then_inc(dn.sem, 1)

            steps(pe, fill, scan_step, tail, rest)


def kernel(L0_attn_x, L0_attn_A_log, L0_attn_D, L0_attn_x_proj_w, L0_attn_dt_proj_w, L0_attn_dt_proj_b,
           L0_ffn_W_up, L0_ffn_W_gate, L0_ffn_W_down, L1_attn_w_qkv, L1_attn_w_out, L1_ffn_w_gate,
           L1_ffn_w_up, L1_ffn_w_down):
    import numpy as np
    import concourse.bacc as bacc
    from concourse.bass_utils import run_bass_kernel_spmd

    B, S, _ = L0_attn_x.shape
    flip = lambda w: np.ascontiguousarray(np.asarray(w).T)
    xp = np.asarray(L0_attn_x_proj_w)
    bc_rows = xp[P:P + 2 * NS]
    xp = np.concatenate([xp[:P], bc_rows, bc_rows, bc_rows, np.zeros_like(bc_rows)], axis=0)
    arrays = {
        "xT": flip(np.asarray(L0_attn_x).reshape(B * S, D)),
        "A_log": np.ascontiguousarray(L0_attn_A_log),
        "Dskip": flip(np.asarray(L0_attn_D).reshape(DH, P)),
        "xprojT": flip(xp),
        "dtT": flip(L0_attn_dt_proj_w),
        "dt_b": flip(np.asarray(L0_attn_dt_proj_b).reshape(DH, P)),
        "wupT": flip(L0_ffn_W_up),
        "wgateT": flip(L0_ffn_W_gate),
        "wdownT": flip(L0_ffn_W_down),
        "wqkvT": flip(L1_attn_w_qkv),
        "woutT": flip(L1_attn_w_out),
        "wgT2": flip(L1_ffn_w_gate),
        "wuT2": flip(L1_ffn_w_up),
        "wdT2": flip(L1_ffn_w_down),
    }
    nc = bacc.Bacc("TRN2", target_bir_lowering=False, num_devices=1)
    args = [nc.dram_tensor(n, a.shape, mybir.dt.from_np(a.dtype), kind="ExternalInput").ap()
            for n, a in arrays.items()]
    out = nc.dram_tensor("out", (B * S, D), F32, kind="ExternalOutput").ap()
    build(nc, *args, out)
    r = run_bass_kernel_spmd(nc, [arrays], core_ids=[0])
    return r.results[0]["out"].reshape(B, S, D)
```

```python
import concourse.bass as bass
from concourse import mybir
from contextlib import ExitStack

F32 = mybir.dt.float32
F32R = mybir.dt.float32r
BF16 = mybir.dt.bfloat16
ALU = mybir.AluOpType
ACT = mybir.ActivationFunctionType
AX = mybir.AxisListType

P = 128
D = 256
DH = D // P
T = 256
TT = T // P
NS = 16
NP = NS // 2
E = 1024
EK = E // P
H = 16
HC = D // H
HG = H // DH
HU = 4
UNITS = H // HU
WIN = T - 64
LN_EPS = 1e-5
Q_EPS = 1e-8
NEG = -1e30
SCALE = 1.0 / float(HC) ** 0.5
RING = 6
PSUM_COLS = 512

ORDER_TEXT = {
    "pe": """
        0.P.dtproj -3.B.out_proj -1.S.spread.6 -2.A.down.0 -3.C.turn.2 -1.S.spread.7 -3.C.ffn.1.0
        -3.C.ffn.1.1 -3.C.ffn.1.2 -3.C.ffn.1.3 -3.C.ffn.1.4 -2.B.turn.1 -3.C.ffn.1.5 0.S.spread.0 -2.B.k
        -2.B.q -2.B.v 0.S.spread.1 -3.C.ffn.1.6 -1.A.turn_in -3.C.ffn.1.7 -2.B.score.0.0 0.S.spread.2
        -2.B.score.0.1 -2.B.score.0.2 -2.B.score.1.0 -2.B.score.1.1 -2.B.score.1.2 -2.B.ptrans.0.0
        -2.B.ptrans.0.1 -2.B.ptrans.0.2 -2.B.score.2.0 -2.B.score.2.1 0.S.spread.3 -2.B.score.2.2 +1.P.xproj
        -2.B.ptrans.1.0 -2.B.ptrans.1.1 0.S.spread.4 -3.C.down.1 -2.B.ptrans.1.2 -2.B.rd.0 -1.A.turn.0
        -2.B.score.3.0 0.S.spread.5 -2.B.score.3.1 -2.B.score.3.2 -2.B.pv.0 -2.B.ptrans.2.0 -2.B.ptrans.2.1
        -2.B.ptrans.2.2 -2.B.ptrans.3.0 -2.B.ptrans.3.1 -1.A.ffn.0.0 -1.A.ffn.0.1 -1.A.ffn.0.2 -1.A.ffn.0.3
        -1.A.ffn.0.4 -1.A.ffn.0.5 -1.A.ffn.0.6 -2.B.ptrans.3.2 -1.A.ffn.0.7 -2.B.rd.1 -2.B.pv.1
    """,
    "act": """
        -3.B.score.2.1 -3.B.score.2.2 -3.B.ptrans.1.0 -1.S.spread.4 -2.A.turn.0 -3.B.ptrans.1.2
        -1.S.spread.5 -3.B.rd.0 -3.B.score.3.0 -3.B.score.3.1 -3.B.score.3.2 -3.B.ptrans.2.0 -3.B.ptrans.2.2
        -3.B.ptrans.3.0 -2.A.ffn.0.0 -2.A.ffn.0.1 -2.A.ffn.0.2 -2.A.ffn.0.3 -2.A.ffn.0.4 -2.A.ffn.0.5
        -3.B.ptrans.3.2 -2.A.ffn.0.6 -3.B.rd.1 -2.A.ffn.0.7 -2.A.split 0.P.dtproj -1.S.spread.6 -3.C.turn.2
        -1.S.spread.7 -3.C.ffn.1.0 -3.C.ffn.1.1 -3.C.ffn.1.2 -3.C.ffn.1.3 -2.B.turn.1 -3.C.ffn.1.4
        -3.C.ffn.1.5 0.S.spread.0 0.S.spread.1 -2.B.q -1.A.turn_in -3.C.ffn.1.6 -3.C.ffn.1.7 0.S.spread.2
        -2.B.score.0.0 -2.B.score.0.1 -2.B.score.0.2 -2.B.score.1.0 -2.B.score.1.1 -2.B.score.1.2
        -2.B.ptrans.0.0 0.S.spread.3 -2.B.ptrans.0.2 -2.B.score.2.0 +1.P.xproj
    """,
    "dve": """
        +1.P.xproj 0.S.state.4 -3.C.down.1 -3.C.norm.3 -1.A.turn.0 -2.B.score.3.0 -2.B.score.3.1
        -2.B.score.3.2 0.S.state.5 -2.B.pv.0 -2.B.ptrans.2.1 -2.B.ptrans.3.1 -1.A.ffn.0.0 -1.A.ffn.0.1
        -1.A.ffn.0.2 -1.A.ffn.0.3 -1.A.ffn.0.4 -1.A.ffn.0.5 -1.A.ffn.0.6 -2.B.pv.1 -1.A.ffn.0.7 -3.C.apply.3
        -1.A.split -2.B.out_proj -2.B.norm.2 +1.P.dtproj -2.B.apply.2 0.S.state.6 -1.A.down.0 -1.A.norm.1
        -2.C.ffn.1.0 0.S.state.7 -1.A.apply.1 -2.C.ffn.1.1 -2.C.ffn.1.2 +1.S.bound -1.B.turn.1 -2.C.ffn.1.3
        -2.C.ffn.1.4 -2.C.ffn.1.5 -1.B.k +1.S.state.0 -1.B.v +1.S.state.1 0.A.norm.0 -2.C.ffn.1.6
        -1.B.score.0.0 -2.C.ffn.1.7 -1.B.score.0.1 -1.B.score.0.2 -1.B.score.1.0 -1.B.score.1.1
        -1.B.score.1.2 +1.S.state.2 -1.B.ptrans.0.1 -1.B.score.2.0 +1.S.state.3 -1.B.score.2.1
        -1.B.score.2.2 -1.B.ptrans.1.1 0.A.apply.0
    """,
    "pool": """
        -1.A.norm.0 0.S.state.1 0.S.state.2 0.S.state.3 0.S.state.4 -3.C.norm.3 -2.B.norm.2 0.S.state.5
        -1.A.norm.1 0.S.state.6 0.S.state.7 +1.S.state.0
    """,
    "sp": """
        -3.B.score.0.0 -3.B.score.1.0 -3.B.score.2.0 -3.B.score.3.0 +1.P.fetch -4.C.apply.3
    """,
}


def pieces_of(text):
    parts = [word.split(".") for word in text.split()]
    return [(int(seq), stage, kind, *map(int, nums)) for seq, stage, kind, *nums in parts]


ORDERS = {engine: pieces_of(text) for engine, text in ORDER_TEXT.items()}
TAKES = ("xproj", "dtproj", "turn_in", "turn", "ffn", "down", "k", "q", "v", "score", "ptrans", "rd", "pv",
         "out_proj")
USES = [p for p in ORDERS["pe"] if p[2] in TAKES]


class Signal:

    def __init__(self, sem, per):
        self.sem, self.per = sem, per

    def wait(self, eng, step, count):
        if isinstance(step, int) and step < 0:
            return
        eng.wait_ge(self.sem, step * self.per + count)


def build(nc, xT, A_log, Dskip, xprojT, dtT, dt_b, wupT, wgateT, wdownT, wqkvT, woutT, wgT2, wuT2, wdT2, out):
    STEPS = xT.shape[1] // T
    with ExitStack() as ctx:
        def sb(name, shape, dt=F32):
            return ctx.enter_context(nc.sbuf_tensor(name, shape, dt))

        w_xp = sb("w_xp", [P, DH, 2 * P])
        w_dt = sb("w_dt", [P, D])
        w_qkv_hi = sb("w_qkv_hi", [P, DH, 3 * D], F32R)
        w_qkv_lo = sb("w_qkv_lo", [P, DH, 3 * D], F32R)
        w_out = sb("w_out", [P, DH, D])
        w_up1 = sb("w_up1", [P, DH, E], F32R)
        w_gate1 = sb("w_gate1", [P, DH, E], F32R)
        w_down1 = sb("w_down1", [P, EK, D], F32R)
        w_gate2 = sb("w_gate2", [P, DH, E])
        w_up2 = sb("w_up2", [P, DH, E])
        w_down2 = sb("w_down2", [P, EK, D])
        ident = sb("ident", [P, P])
        ident_b = sb("ident_b", [P, P], BF16)
        pick = sb("pick", [P, 2 * NS], BF16)
        mask0 = sb("mask0", [P, P], BF16)
        mask1 = sb("mask1", [P, WIN], BF16)
        ones = sb("ones", [P, P])
        half_neg = sb("half_neg", [P, TT])
        A_neg = sb("A_neg", [P, DH, NS])
        d_one = sb("d_one", [P, DH])
        b_dt = sb("b_dt", [P, DH])
        q_sum = sb("q_sum", [P, 4])
        q_thr = sb("q_thr", [P, 8])
        x_ch = sb("x_ch", [P, DH, T])
        dr = sb("dr", [P, T])
        z_pos = sb("z_pos", [P, DH, T])
        z_log = sb("z_log", [P, DH, T])
        bc_next = sb("bc_next", [P, T], BF16)
        bc_rest = sb("bc_rest", [P, T])
        bc_mid = sb("bc_mid", [P, T], BF16)
        bc_parts = sb("bc_parts", [P, T], BF16)
        delta = sb("delta", [P, DH, T])
        du = sb("du", [P, DH, T])
        x_skip = sb("x_skip", [P, DH, T])
        dA = sb("dA", [P, 2, 2, DH, T])
        hs = sb("hs", [P, 3, 2, DH, T])
        cs = sb("cs", [P, 2, 2, T])
        r_ch = sb("r_ch", [P, DH, T])
        r_tok = sb("r_tok", [P, TT, D])
        x_tok = [sb(f"x_tok{k}", [P, TT, D]) for k in range(4)]
        stats = sb("stats", [P, 4, TT, 6])
        mv = sb("mv", [P, 4, TT, 2])
        var_eps = sb("var_eps", [P, 4, TT])
        rstd = sb("rstd", [P, 4, TT])
        pause = sb("pause", [P, 1])
        x_hi = [sb(f"x_hi{k}", [P, DH, T], F32R) for k in range(2)]
        x_lo = [sb(f"x_lo{k}", [P, DH, T], F32R) for k in range(2)]
        x_t = sb("x_t", [P, DH, T])
        th = sb("th", [P, 2, 2, T])
        hid = sb("hid", [P, 2, 2, T])
        at_hidden = nc.sbuf_base
        h_hi = sb("h_hi", [P, EK, T], F32R)
        h_lo = sb("h_lo", [P, EK, T], F32R)
        h2 = sb("h2", [P, EK, T])
        q_ch = sb("q_ch", [P, DH, T])
        k_ch = sb("k_ch", [P, DH, T])
        Kx = sb("Kx", [P, 2, HU, T])
        Vz = sb("Vz", [P, TT, H, 2 * HC])
        nb = sb("nb", [P, 2, 2, 2, HU])
        den = sb("den", [P, DH, TT, HG])
        rden = sb("rden", [P, TT, HG])
        rden_x = sb("rden_x", [P, TT, HG, HC])
        P0 = sb("P0", [P, 2, HU, P])
        P1 = sb("P1", [P, 2, HU, T])
        at_turned = nc.sbuf_base
        PT0 = sb("PT0", [P, 2, HU, T])
        PT1 = sb("PT1", [P, 2, HU, P])
        rd_ch = sb("rd_ch", [P, T])
        o_ch = sb("o_ch", [P, DH, T])
        w_raw = nc.alloc_sbuf_tensor_at("w_raw", [P, 3, 2 * E], F32, offset=at_hidden)
        qkv_raw = nc.alloc_sbuf_tensor_at("qkv_raw", [P, DH, 3 * D], F32, offset=at_turned)
        w_low = hs[:, 0:2].rearrange("p a n h t -> p (a n h t)")

        ps = [ctx.enter_context(nc.psum_tensor(f"ps{i}", [P, PSUM_COLS], F32)) for i in range(8)]
        bankB, bankC, ring = ps[0], ps[1], ps[2:]

        def sem(name):
            return ctx.enter_context(nc.semaphore(name))

        def sig(name, per):
            return Signal(sem(name), per)

        s_load = [sem(f"loaded_{n}") for n in range(5)]
        s_const = sem("const_made")
        s_prep = sem("prep_vector")
        s_preps = sem("prep_scalar")
        s_prept = sem("prep_tensor")
        CONST_ALL, PREP_ALL = 21, 15
        x_in = sig("x_loaded", 16)
        xdbl = sig("xdbl_made", 1)
        drc = sig("dr_copied", 2)
        bcs = sig("bc_split", 4)
        dtp = sig("dt_made", 1)
        sp = sig("softplus_steps", 3)
        zp = sig("z_positive", 1)
        bd = sig("scan_inputs", 4)
        bb = sig("B_spread", NP)
        bc = sig("C_spread", NP)
        exa = sig("dA_made", NP)
        ccp = sig("C_copied", NP)
        dbu = sig("dBu_made", NP)
        scn = sig("scanned", NP)
        hc = sig("y_steps", 3 * NP)
        tra = sig("r_turned", 1)
        rtc = sig("r_copied", 1)
        dn = [None] + [sig(f"projected_{k}", 1) for k in (1, 2, 3)]
        rr = [None] + [sig(f"residual_added_{k}", 1) for k in (1, 2, 3)]
        st = [sig(f"stats_steps_{k}", 3) for k in range(4)]
        pw = [sig(f"rstd_made_{k}", 1) for k in range(4)]
        xn = [sig(f"normed_{k}", 1) for k in range(4)]
        trx = [sig(f"x_turned_{k}", 1) for k in range(3)]
        xh = [sig(f"x_high_{k}", 1) for k in range(2)]
        xl = [sig(f"x_low_{k}", 1) for k in range(2)]
        xe = sig("x_copied", 1)
        ug = [sig(f"up_gate_made_{f}", EK) for f in range(2)]
        thd = [sig(f"tanh_made_{f}", EK) for f in range(2)]
        mmd = [sig(f"silu_made_{f}", EK) for f in range(2)]
        hd = [sig(f"hidden_made_{f}", EK) for f in range(2)]
        hh = sig("hidden_high", EK // 2)
        hl = sig("hidden_low", EK // 2)
        qm, km, vm = sig("q_made", 1), sig("k_made", 1), sig("v_made", 1)
        qc, kc, vz = sig("q_copied", 1), sig("k_copied", 1), sig("v_copied", 2)
        kx = [sig(f"k_spread_{u}", 16 * HU) for u in range(UNITS)]
        sc = sig("scores_made", 3 * UNITS)
        nbs = sig("max_steps", 6 * UNITS)
        ex = sig("exps_made", 3 * UNITS)
        tt = sig("probs_turned", 3 * UNITS)
        ptd = sig("pt_copied_vector", UNITS)
        pta = sig("pt_copied_scalar", 2 * UNITS)
        rds = sig("rden_made", 2 * DH)
        rdt = sig("rden_turned", DH)
        rdc = sig("rden_copied", DH)
        pv = sig("pv_made", DH)
        ot = sig("o_made", DH)
        odma = sig("stored", 16)

        def freed(kind, *at):
            if kind == "xproj":
                return bcs, 1
            if kind == "dtproj":
                return zp, 1
            if kind == "turn_in":
                return rtc, 1
            if kind == "turn":
                return (xl[0], xl[1], xe)[at[0]], 1
            if kind == "ffn":
                return hd[at[0]], at[1] + 1
            if kind == "down":
                return rr[(1, 3)[at[0]]], 1
            if kind == "out_proj":
                return rr[2], 1
            if kind == "score":
                return ex, 3 * at[0] + at[1] + 1
            if kind == "ptrans":
                return (ptd, at[0] + 1) if at[1] == 1 else (pta, 2 * at[0] + 1 + at[1] // 2)
            return {"q": (qc, 1), "k": (kc, 1), "v": (vz, 2), "rd": (rdc, at[0] + 1 if at else 0),
                    "pv": (ot, at[0] + 1 if at else 0)}[kind]

        def use(stage, *piece):
            return [p[1:] for p in USES].index((stage, *piece))

        def bank(stage, *piece):
            return ring[use(stage, *piece) % RING]

        def take(it, stage, *piece):
            n = use(stage, *piece)
            slot, held_by = n % RING, n - RING
            while True:
                if held_by < 0:
                    it, held_by = it - 1, max(m for m in range(len(USES)) if m % RING == slot)
                ahead, _, *before = USES[held_by]
                if not isinstance(it, int) or present(it + ahead):
                    signal, count = freed(*before)
                    signal.wait(nc.tensor, it + ahead, count)
                    break
                if it < -max(p[0] for p in USES):
                    break
                held_by -= RING
            return ring[slot]

        def present(j):
            return 0 <= j < STEPS

        def iterations(eng, which, piece):
            ahead = [p[0] for p in ORDERS[which]]

            def one(it):
                for rel, _, kind, *at in ORDERS[which]:
                    if not isinstance(it, int) or present(it + rel):
                        piece(it, it + rel, kind, *at)

            loop = 1 - min(ahead), STEPS - max(ahead)
            for it in range(-max(ahead), loop[0]):
                one(it)
            with eng.Fori(*loop) as it:
                one(it)
            for it in range(loop[1], STEPS - min(ahead)):
                one(it)

        block = ctx.enter_context(nc.Block())

        @block.sync
        def _(sp_):
            def load(dst, src, lot):
                sp_.dma_start(dst, src).then_inc(s_load[lot], 16)

            load(w_xp[:], xprojT.rearrange("(k p) e -> p k e", p=P), 0)
            sp_.dma_start(x_ch[:], xT[:, 0:T].rearrange("(k p) t -> p k t", p=P)).then_inc(x_in.sem, 16)
            load(w_dt[:], dtT, 0)
            load(A_neg[:], A_log.rearrange("(k p) n -> p k n", p=P), 2)
            load(d_one[:], Dskip, 2)
            load(b_dt[:], dt_b, 2)
            for n, (w, rows) in enumerate(((wupT, DH), (wgateT, DH), (wdownT, EK))):
                load(w_raw[:, n, :].rearrange("p (k e) -> p k e", k=rows),
                     w.rearrange("(k p) e -> p k e", p=P), 1)
            load(qkv_raw[:], wqkvT.rearrange("(k p) e -> p k e", p=P), 4)
            for dst, w in ((w_out, woutT), (w_gate2, wgT2), (w_up2, wuT2), (w_down2, wdT2)):
                load(dst[:], w.rearrange("(k p) e -> p k e", p=P), 3)

            def piece(it, j, kind, *at):
                rows = slice(j * T, (j + 1) * T) if isinstance(j, int) else None
                if kind == "fetch" and not (isinstance(j, int) and j == 0):
                    rows = rows or bass.ds(sp_.snap(j * T), T)
                    bd.wait(sp_, j - 1, 4)
                    sp_.dma_start(x_ch[:], xT[:, rows].rearrange("(k p) t -> p k t", p=P)
                                  ).then_inc(x_in.sem, 16)
                elif kind == "score":
                    u = at[0]
                    g, half = divmod(u, 2)
                    if u < 2:
                        kc.wait(sp_, j, 1)
                    else:
                        sc.wait(sp_, j, 3 * (u - 1))
                    for h in range(HU):
                        own = slice((half * HU + h) * HC, (half * HU + h + 1) * HC)
                        sp_.dma_start(Kx[own, u % 2, h, :], k_ch[own, g, :]).then_inc(kx[u].sem, 16)
                elif kind == "apply":
                    rows = rows or bass.ds(sp_.snap(j * T), T)
                    xn[3].wait(sp_, j, 1)
                    sp_.dma_start(out[rows, :].rearrange("(t p) d -> p t d", p=P), x_tok[3][:]
                                  ).then_inc(odma.sem, 16)

            iterations(sp_, "sp", piece)
            odma.wait(sp_, STEPS - 1, 16)

        @block.gpsimd
        def _(pool):
            for t, v in ((ident, 0.0), (ident_b, 0.0), (pick, 0.0), (mask0, 0.0), (mask1, 0.0), (ones, 1.0),
                         (half_neg, -0.5)):
                pool.memset(t[:], v).then_inc(s_const, 1)
            pool.wait_ge(s_const, 7)
            for t in (ident, ident_b):
                pool.affine_select(out=t[:], in_=t[:], compare_op=ALU.not_equal, fill=1.0, base=0,
                                   pattern=[[-1, P]], channel_multiplier=1).then_inc(s_const, 1)
            for c in range(3):
                pool.affine_select(out=pick[:], in_=pick[:], compare_op=ALU.not_equal, fill=1.0, base=-32 * c,
                                   pattern=[[-1, 2 * NS]], channel_multiplier=1).then_inc(s_const, 1)
                pool.wait_ge(s_const, 10 + c)
            for m, w, lo in ((mask0, P, 0), (mask1, WIN, 64)):
                pool.affine_select(out=m[:], in_=m[:], compare_op=ALU.is_ge, fill=NEG, base=lo,
                                   pattern=[[-1, w]], channel_multiplier=1).then_inc(s_const, 1)
            pool.wait_ge(s_const, 14)
            for m, w, lo in ((mask0, P, 0), (mask1, WIN, 64)):
                pool.affine_select(out=m[:], in_=m[:], compare_op=ALU.is_ge, fill=NEG, base=64 - lo,
                                   pattern=[[1, w]], channel_multiplier=-1).then_inc(s_const, 1)
            for n in range(2):
                pool.memset(dA[:, n, :, :, 0:1], 0.0).then_inc(s_const, 1)
            pool.memset(Kx[:], 0.0).then_inc(s_const, 1)
            pool.memset(Vz[:], 0.0).then_inc(s_const, 1)
            pool.memset(P1[:, :, :, 0:T - WIN], 0.0).then_inc(s_const, 1)

            def piece(it, j, kind, *at):
                if kind == "state":
                    n = at[0]
                    scn.wait(pool, j, n + 1)
                    ccp.wait(pool, j, n + 1)
                    pool.tensor_tensor(hs[:, n % 3], hs[:, n % 3],
                                       cs[:, n % 2].unsqueeze(2).broadcast_to([P, 2, DH, T]), ALU.mult
                                       ).then_inc(hc.sem, 1)
                    hc.wait(pool, j, 3 * n + 1)
                    if n == 0:
                        bd.wait(pool, j, 4)
                        tra.wait(pool, j - 1, 1)
                    pool.tensor_tensor(r_ch[:], (x_skip if n == 0 else r_ch)[:], hs[:, n % 3, 0], ALU.add
                                       ).then_inc(hc.sem, 1)
                    hc.wait(pool, j, 3 * n + 2)
                    pool.tensor_tensor(r_ch[:], r_ch[:], hs[:, n % 3, 1], ALU.add).then_inc(hc.sem, 1)
                elif kind == "norm":
                    k = at[0]
                    st[k].wait(pool, j, 3)
                    pool.tensor_tensor(rstd[:, k], var_eps[:, k], half_neg[:], ALU.pow).then_inc(pw[k].sem, 1)

            iterations(pool, "pool", piece)

        @block.scalar
        def _(act):
            act.wait_ge(s_load[2], 48)
            act.activation(A_neg[:], A_neg[:], ACT.Exp).then_inc(s_preps, 1)
            act.wait_ge(s_load[1], 48)
            for n in range(3):
                act.activation(w_low, w_raw[:, n], ACT.Abs, accum_out=q_sum[:, n:n + 1]).then_inc(s_preps, 1)
                act.wait_ge(s_preps, 2 + n)
            act.wait_ge(s_load[4], 16)
            act.activation(w_qkv_hi[:], qkv_raw[:], ACT.Copy).then_inc(s_preps, 1)
            act.wait_ge(s_const, CONST_ALL)
            act.wait_ge(s_prep, PREP_ALL)

            def piece(it, j, kind, *at):
                if kind == "xproj":
                    pb = bank("P", kind)
                    xdbl.wait(act, j, 1)
                    act.activation(dr[:], pb[:, 0:T], ACT.Copy).then_inc(drc.sem, 1)
                    bd.wait(act, j - 1, 1)
                    act.activation(bc_next[:], pb[:, T:2 * T], ACT.Copy).then_inc(drc.sem, 1)
                elif kind == "dtproj":
                    dtp.wait(act, j, 1)
                    bd.wait(act, j - 1, 2)
                    for h in range(DH):
                        last = act.activation(z_log[:, h], bank("P", kind)[:, h * T:(h + 1) * T], ACT.Abs,
                                              bias=b_dt[:, h:h + 1])
                    last.then_inc(sp.sem, 1)
                    sp.wait(act, j, 1)
                    act.activation(z_log[:], z_log[:], ACT.Exp, scale=-1.0).then_inc(sp.sem, 1)
                    sp.wait(act, j, 2)
                    act.activation(z_log[:], z_log[:], ACT.Ln, bias=1.0).then_inc(sp.sem, 1)
                elif kind == "spread":
                    n = at[0]
                    if n == 0:
                        bd.wait(act, j, 2)
                    if n >= 2:
                        scn.wait(act, j, n - 1)
                    else:
                        scn.wait(act, j - 1, NP - 1 + n)
                    for m in range(2):
                        for h in range(DH):
                            last = act.activation(dA[:, n % 2, m, h, 1:], delta[:, h, 1:], ACT.Exp,
                                                  scale=A_neg[:, h, 2 * n + m:2 * n + m + 1])
                    last.then_inc(exa.sem, 1)
                    bc.wait(act, j, n + 1)
                    if n >= 2:
                        hc.wait(act, j, 3 * (n - 2) + 1)
                    else:
                        hc.wait(act, j - 1, 3 * (NP - 2 + n) + 1)
                    act.activation(cs[:, n % 2].rearrange("p m t -> p (m t)"), bankC[:], ACT.Copy
                                   ).then_inc(ccp.sem, 1)
                elif kind == "turn_in":
                    tra.wait(act, j, 1)
                    xn[0].wait(act, j - 1, 1)
                    act.activation(r_tok[:].rearrange("p t d -> p (t d)"), bank("A", kind)[:], ACT.Copy
                                   ).then_inc(rtc.sem, 1)
                elif kind == "turn":
                    k = at[0]
                    src = bank("ABC"[k], kind, k)[:]
                    trx[k].wait(act, j, 1)
                    if k < 2:
                        act.activation(x_hi[k][:].rearrange("p k t -> p (k t)"), src, ACT.Copy
                                       ).then_inc(xh[k].sem, 1)
                    else:
                        act.activation(x_t[:].rearrange("p k t -> p (k t)"), src, ACT.Copy
                                       ).then_inc(xe.sem, 1)
                elif kind == "ffn":
                    f, e = at
                    ug[f].wait(act, j, e + 1)
                    if e >= 2:
                        hd[f].wait(act, j, e - 1)
                    act.activation(th[:, f, e % 2], bank("AC"[f], kind, f, e)[:, 0:T], ACT.Tanh,
                                   scale=q_thr[:, 6:7] if f == 0 else 0.5).then_inc(thd[f].sem, 1)
                    if f == 0 and e % 2 == 0 and e:
                        high(j, e // 2 - 1)
                elif kind == "split":
                    high(j, EK // 2 - 1)
                elif kind == "q":
                    qm.wait(act, j, 1)
                    act.activation(q_ch[:].rearrange("p k t -> p (k t)"), bank("B", kind)[:], ACT.Copy
                                   ).then_inc(qc.sem, 1)
                elif kind == "score":
                    u, b = at
                    g, half = divmod(u, 2)
                    nbs.wait(act, j, 6 * u + 2 * b + 2)
                    if b == 0 and u >= 2:
                        tt.wait(act, j, 3 * (u - 1))
                    q, heads, wid = (0, range(HU), P) if b == 0 else (1, range(2 * b - 2, 2 * b), WIN)
                    for n, h in enumerate(heads):
                        dst = P0[:, u % 2, h] if b == 0 else P1[:, u % 2, h, T - WIN:T]
                        last = act.activation(dst, bank("B", kind, u, b)[:, n * wid:(n + 1) * wid], ACT.Exp,
                                              scale=SCALE, bias=nb[:, u % 2, 1, q, h:h + 1],
                                              accum_out=den[:, g, q, half * HU + h:half * HU + h + 1])
                    last.then_inc(ex.sem, 1)
                elif kind == "ptrans" and at[1] != 1:
                    u, b = at
                    tt.wait(act, j, 3 * u + b + 1)
                    if u >= 2 and b == 0:
                        pv.wait(act, j, 1)
                    dst = PT0[:, u % 2, 0:2] if b == 0 else PT1[:, u % 2]
                    act.activation(dst.rearrange("p a b -> p (a b)"), bank("B", kind, u, b)[:], ACT.Copy
                                   ).then_inc(pta.sem, 1)
                elif kind == "rd":
                    g = at[0]
                    rdt.wait(act, j, g + 1)
                    if g:
                        ot.wait(act, j, g)
                    act.activation(rd_ch[:], bank("B", kind, g)[:, 0:T], ACT.Copy).then_inc(rdc.sem, 1)

            def high(j, pair):
                hd[0].wait(act, j, 2 * pair + 2)
                act.activation(h_hi[:, 2 * pair:2 * pair + 2], hid[:, pair % 2], ACT.Copy).then_inc(hh.sem, 1)

            iterations(act, "act", piece)

        @block.vector
        def _(dve):
            dve.wait_ge(s_preps, 1)
            dve.tensor_scalar(A_neg[:], A_neg[:], -1.0, None, ALU.mult).then_inc(s_prep, 1)
            dve.tensor_scalar(d_one[:], d_one[:], 1.0, None, ALU.add).then_inc(s_prep, 1)
            dve.wait_ge(s_prept, 1)
            dve.tensor_scalar(q_sum[:, 0:3], ring[0][:, 0:3], 1.0 / (D * E), Q_EPS, ALU.mult, ALU.add
                              ).then_inc(s_prep, 1)
            dve.wait_ge(s_prep, 3)
            dve.tensor_scalar(q_thr[:, 0:3], q_sum[:, 0:3], 0.5, None, ALU.mult).then_inc(s_prep, 1)
            dve.tensor_scalar(q_thr[:, 3:6], q_sum[:, 0:3], -0.5, None, ALU.mult).then_inc(s_prep, 1)
            dve.wait_ge(s_prep, 5)
            dve.tensor_scalar(q_thr[:, 6:7], q_thr[:, 0:1], 1.0, None, ALU.mult).then_inc(s_prep, 1)
            dve.tensor_tensor(q_thr[:, 7:8], q_thr[:, 0:1], q_sum[:, 1:2], ALU.mult).then_inc(s_prep, 1)
            dve.wait_ge(s_prep, 7)
            dve.tensor_tensor(q_thr[:, 7:8], q_thr[:, 7:8], q_sum[:, 2:3], ALU.mult).then_inc(s_prep, 1)
            dve.wait_ge(s_preps, 4)
            for n, w in enumerate((w_up1, w_gate1, w_down1)):
                if n:
                    dve.wait_ge(s_prep, 8 + 2 * n)
                dve.tensor_scalar(w_low, w_raw[:, n], q_thr[:, 3 + n:4 + n], None, ALU.is_lt).then_inc(s_prep, 1)
                dve.wait_ge(s_prep, 9 + 2 * n)
                dve.scalar_tensor_tensor(w[:].rearrange("p k e -> p (k e)"), w_raw[:, n], q_thr[:, n:n + 1],
                                         w_low, ALU.is_gt, ALU.subtract).then_inc(s_prep, 1)
            dve.wait_ge(s_preps, 5)
            dve.tensor_tensor(w_qkv_lo[:], qkv_raw[:], w_qkv_hi[:].bitcast(F32), ALU.subtract
                              ).then_inc(s_prep, 1)
            dve.wait_ge(s_prep, PREP_ALL)
            dve.wait_ge(s_const, CONST_ALL)

            def piece(it, j, kind, *at):
                if kind == "xproj":
                    drc.wait(dve, j, 2)
                    dve.tensor_tensor(bc_rest[:], bank("P", kind)[:, T:2 * T], bc_next[:], ALU.subtract
                                      ).then_inc(bcs.sem, 1)
                    bcs.wait(dve, j, 1)
                    dve.tensor_copy(bc_next[32:64], bc_rest[32:64]).then_inc(bcs.sem, 1)
                    dve.tensor_copy(bc_mid[64:96], bc_rest[64:96]).then_inc(bcs.sem, 1)
                    bcs.wait(dve, j, 3)
                    dve.tensor_tensor(bc_next[64:96], bc_rest[64:96], bc_mid[64:96], ALU.subtract
                                      ).then_inc(bcs.sem, 1)
                elif kind == "dtproj":
                    sp.wait(dve, j, 1)
                    for h in range(DH):
                        last = dve.tensor_scalar(z_pos[:, h], bank("P", kind)[:, h * T:(h + 1) * T],
                                                 b_dt[:, h:h + 1], 0.0, ALU.add, ALU.max)
                    last.then_inc(zp.sem, 1)
                elif kind == "bound":
                    bcs.wait(dve, j, 4)
                    bb.wait(dve, j - 1, NP)
                    bc.wait(dve, j - 1, NP)
                    dve.tensor_copy(bc_parts[:], bc_next[:]).then_inc(bd.sem, 1)
                    sp.wait(dve, j, 3)
                    zp.wait(dve, j, 1)
                    exa.wait(dve, j - 1, NP)
                    dve.tensor_tensor(delta[:], z_pos[:], z_log[:], ALU.add).then_inc(bd.sem, 1)
                    bd.wait(dve, j, 2)
                    x_in.wait(dve, j, 16)
                    dve.tensor_tensor(du[:], delta[:], x_ch[:], ALU.mult).then_inc(bd.sem, 1)
                    hc.wait(dve, j - 1, 2)
                    for h in range(DH):
                        last = dve.tensor_scalar(x_skip[:, h], x_ch[:, h], d_one[:, h:h + 1], None, ALU.mult)
                    last.then_inc(bd.sem, 1)
                elif kind == "state":
                    n = at[0]
                    if n == 0:
                        bd.wait(dve, j, 3)
                    bb.wait(dve, j, n + 1)
                    if n >= 3:
                        hc.wait(dve, j, 3 * (n - 2))
                    else:
                        last = max(m for m in range(NP) if m % 3 == n)
                        hc.wait(dve, j - 1, 3 * (last + 1))
                    dve.tensor_tensor(hs[:, n % 3], du[:].unsqueeze(1).broadcast_to([P, 2, DH, T]),
                                      bankB[:].rearrange("p (m t) -> p m t", m=2).unsqueeze(2)
                                      .broadcast_to([P, 2, DH, T]), ALU.mult).then_inc(dbu.sem, 1)
                    dbu.wait(dve, j, n + 1)
                    exa.wait(dve, j, n + 1)
                    flat = hs[:, n % 3].rearrange("p m h t -> p (m h t)")
                    dve.tensor_tensor_scan(flat, dA[:, n % 2].rearrange("p m h t -> p (m h t)"), flat, 0.0,
                                           ALU.mult, ALU.add).then_inc(scn.sem, 1)
                elif kind == "norm":
                    k = at[0]
                    if k:
                        rr[k].wait(dve, j, 1)
                    else:
                        rtc.wait(dve, j, 1)
                    for t in range(TT):
                        last = dve.bn_stats(stats[:, k, t], rows_in(k, t))
                    last.then_inc(st[k].sem, 1)
                    st[k].wait(dve, j, 1)
                    dve.memset(pause[:], 0.0)
                    for t in range(TT):
                        last = dve.bn_aggr(mv[:, k, t], stats[:, k, t])
                    last.then_inc(st[k].sem, 1)
                    st[k].wait(dve, j, 2)
                    dve.tensor_scalar(var_eps[:, k], mv[:, k, :, 1], LN_EPS, None, ALU.add
                                      ).then_inc(st[k].sem, 1)
                elif kind == "apply":
                    k = at[0]
                    pw[k].wait(dve, j, 1)
                    if k < 3:
                        xn[k + 1].wait(dve, j - 1, 1)
                    if k == 3:
                        odma.wait(dve, j - 1, 16)
                    for t in range(TT):
                        last = dve.tensor_scalar(x_tok[k][:, t], rows_in(k, t), mv[:, k, t, 0:1],
                                                 rstd[:, k, t:t + 1], ALU.subtract, ALU.mult)
                    last.then_inc(xn[k].sem, 1)
                elif kind == "turn" and at[0] < 2:
                    k = at[0]
                    xh[k].wait(dve, j, 1)
                    dve.tensor_tensor(x_lo[k][:].rearrange("p k t -> p (k t)"), bank("AB"[k], kind, k)[:],
                                      x_hi[k][:].rearrange("p k t -> p (k t)").bitcast(F32), ALU.subtract
                                      ).then_inc(xl[k].sem, 1)
                elif kind == "ffn":
                    f, e = at
                    pb = bank("AC"[f], kind, f, e)
                    thd[f].wait(dve, j, e + 1)
                    m = th[:, f, e % 2]
                    dve.scalar_tensor_tensor(m, m, 1.0, pb[:, 0:T], ALU.add, ALU.mult).then_inc(mmd[f].sem, 1)
                    mmd[f].wait(dve, j, e + 1)
                    if f == 0 and e >= 4 and e % 2 == 0:
                        hl.wait(dve, j, e // 2 - 1)
                    dst = hid[:, (e // 2) % 2, e % 2] if f == 0 else h2[:, e]
                    dve.tensor_tensor(dst, m, pb[:, T:2 * T], ALU.mult).then_inc(hd[f].sem, 1)
                    if f == 0 and e % 2 == 0 and e:
                        low(j, e // 2 - 1)
                elif kind == "split":
                    low(j, EK // 2 - 1)
                elif kind in ("down", "out_proj"):
                    stage, k = {("down", 0): ("A", 1), ("out_proj",): ("B", 2), ("down", 1): ("C", 3)}[(kind, *at)]
                    x = x_tok[k - 1][:].rearrange("p a b -> p (a b)")
                    dn[k].wait(dve, j, 1)
                    dve.scalar_tensor_tensor(x, bank(stage, kind, *at)[:], (q_thr[:, 7:8], 1.0, 0.5)[k - 1], x,
                                             ALU.mult, ALU.add).then_inc(rr[k].sem, 1)
                elif kind == "k":
                    km.wait(dve, j, 1)
                    dve.tensor_copy(k_ch[:].rearrange("p k t -> p (k t)"), bank("B", kind)[:]
                                    ).then_inc(kc.sem, 1)
                elif kind == "v":
                    vm.wait(dve, j, 1)
                    dst = Vz[:].rearrange("p t (a o) d -> p t a o d", o=2)
                    src = bank("B", kind)[:].rearrange("p (t a o d) -> p t a o d", t=TT, a=H // 2, o=2)
                    for odd in range(2):
                        dve.tensor_copy(dst[:, :, :, odd, HC * odd:HC * odd + HC], src[:, :, :, odd, :]
                                        ).then_inc(vz.sem, 1)
                elif kind == "score":
                    u, b = at
                    sc.wait(dve, j, 3 * u + b + 1)
                    q, h0, n, wid = (0, 0, HU, P) if b == 0 else (1, 2 * b - 2, 2, WIN)
                    dve.tensor_reduce(nb[:, u % 2, 0, q, h0:h0 + n],
                                      bank("B", kind, u, b)[:, :n * wid].rearrange("p (n w) -> p n w", n=n),
                                      AX.X, ALU.max).then_inc(nbs.sem, 1)
                    nbs.wait(dve, j, 6 * u + 2 * b + 1)
                    dve.tensor_scalar(nb[:, u % 2, 1, q, h0:h0 + n], nb[:, u % 2, 0, q, h0:h0 + n], -SCALE,
                                      None, ALU.mult).then_inc(nbs.sem, 1)
                elif kind == "ptrans" and at[1] == 1:
                    u = at[0]
                    tt.wait(dve, j, 3 * u + 2)
                    if u >= 2:
                        pv.wait(dve, j, 1)
                    dve.tensor_copy(PT0[:, u % 2, 2:4].rearrange("p a b -> p (a b)"),
                                    bank("B", kind, u, 1)[:]).then_inc(ptd.sem, 1)
                    if u % 2:
                        g = u // 2
                        dve.reciprocal(rden[:].rearrange("p q h -> p (q h)"),
                                       den[:, g].rearrange("p q h -> p (q h)")).then_inc(rds.sem, 1)
                        rds.wait(dve, j, 2 * g + 1)
                        rdt.wait(dve, *((j, g) if g else (j - 1, DH)))
                        dve.tensor_copy(rden_x[:].rearrange("p q h c -> p (q h) c"),
                                        rden[:].rearrange("p q h -> p (q h)").unsqueeze(2)
                                        .broadcast_to([P, TT * HG, HC])).then_inc(rds.sem, 1)
                elif kind == "pv":
                    g = at[0]
                    rdc.wait(dve, j, g + 1)
                    pv.wait(dve, j, g + 1)
                    dve.tensor_tensor(o_ch[:, g], bank("B", kind, g)[:, 0:T], rd_ch[:], ALU.mult
                                      ).then_inc(ot.sem, 1)

            def low(j, pair):
                hh.wait(dve, j, pair + 1)
                dve.tensor_tensor(h_lo[:, 2 * pair:2 * pair + 2], hid[:, pair % 2],
                                  h_hi[:, 2 * pair:2 * pair + 2].bitcast(F32), ALU.subtract
                                  ).then_inc(hl.sem, 1)

            def rows_in(k, t):
                return (r_tok if k == 0 else x_tok[k - 1])[:, t]

            iterations(dve, "dve", piece)

        @block.tensor
        def _(pe):
            pe.wait_ge(s_preps, 4)
            pe.wait_ge(s_const, 7)
            nc.tensor.matmul(ring[0][:, 0:3], ones[:], q_sum[:, 0:3], start=True, stop=True).then_inc(s_prept, 1)
            pe.wait_ge(s_load[0], 32)
            pe.wait_ge(s_load[3], 64)
            pe.wait_ge(s_const, CONST_ALL)
            pe.wait_ge(s_prep, PREP_ALL)

            def acc(dst, pairs):
                for n, (l, r) in enumerate(pairs):
                    last = nc.tensor.matmul(dst, l, r, start=n == 0, stop=n == len(pairs) - 1)
                return last

            def piece(it, j, kind, *at):
                if kind == "xproj":
                    x_in.wait(pe, j, 16)
                    pb = take(it, "P", kind)
                    for m in range(2):
                        last = acc(pb[:, m * T:(m + 1) * T],
                                   [(w_xp[:, k, m * P:(m + 1) * P], x_ch[:, k]) for k in range(DH)])
                    last.then_inc(xdbl.sem, 1)
                elif kind == "dtproj":
                    drc.wait(pe, j, 1)
                    pb = take(it, "P", kind)
                    for h in range(DH):
                        last = acc(pb[:, h * T:(h + 1) * T], [(w_dt[:, h * P:(h + 1) * P], dr[:])])
                    last.then_inc(dtp.sem, 1)
                elif kind == "spread":
                    n = at[0]
                    if n == 0:
                        bd.wait(pe, j, 1)
                    for base, dst, used, done in ((0, bankB, dbu, bb), (NS, bankC, ccp, bc)):
                        used.wait(pe, *((j, n) if n else (j - 1, NP)))
                        for m in range(2):
                            row = base + 2 * n + m
                            last = nc.tensor.matmul(dst[:, m * T:(m + 1) * T],
                                                    pick[:, row:row + 1].broadcast_to([P, P]), bc_parts[:],
                                                    start=True, stop=True)
                        last.then_inc(done.sem, 1)
                elif kind == "turn_in":
                    hc.wait(pe, j, 3 * NP)
                    pb = take(it, "A", kind)
                    for t in range(TT):
                        for c in range(DH):
                            last = nc.tensor.transpose(pb[:, t * D + c * P:t * D + (c + 1) * P],
                                                       r_ch[:, c, t * P:(t + 1) * P], ident[:])
                    last.then_inc(tra.sem, 1)
                elif kind == "turn":
                    k = at[0]
                    xn[k].wait(pe, j, 1)
                    pb = take(it, "ABC"[k], kind, k)
                    for c in range(DH):
                        for t in range(TT):
                            last = nc.tensor.transpose(pb[:, c * T + t * P:c * T + (t + 1) * P],
                                                       x_tok[k][:, t, c * P:(c + 1) * P], ident[:])
                    last.then_inc(trx[k].sem, 1)
                elif kind == "ffn":
                    f, e = at
                    if e == 0:
                        (xl[0] if f == 0 else xe).wait(pe, j, 1)
                    pb = take(it, "AC"[f], kind, f, e)
                    cols = slice(e * P, (e + 1) * P)
                    for n in range(2):
                        if f == 0:
                            w = (w_up1, w_gate1)[n]
                            pairs = [(w[:, k, cols], x[:, k]) for k in range(DH) for x in (x_lo[0], x_hi[0])]
                        else:
                            w = (w_gate2, w_up2)[n]
                            pairs = [(w[:, k, cols], x_t[:, k]) for k in range(DH)]
                        last = acc(pb[:, n * T:(n + 1) * T], pairs)
                    last.then_inc(ug[f].sem, 1)
                elif kind == "down":
                    f = at[0]
                    if f == 0:
                        hl.wait(pe, j, EK // 2)
                    else:
                        hd[1].wait(pe, j, EK)
                    pb = take(it, "AC"[f], kind, f)
                    for t in range(TT):
                        rows = slice(t * P, (t + 1) * P)
                        if f == 0:
                            pairs = [(x[:, e, rows], w_down1[:, e]) for e in range(EK) for x in (h_lo, h_hi)]
                        else:
                            pairs = [(h2[:, e, rows], w_down2[:, e]) for e in range(EK)]
                        last = acc(pb[:, t * D:(t + 1) * D], pairs)
                    last.then_inc(dn[(1, 3)[f]].sem, 1)
                elif kind in ("q", "k"):
                    if kind == "k":
                        xl[1].wait(pe, j, 1)
                    pb = take(it, "B", kind)
                    for g in range(DH):
                        cols = slice((D if kind == "k" else 0) + g * P, (D if kind == "k" else 0) + (g + 1) * P)
                        last = acc(pb[:, g * T:(g + 1) * T],
                                   [(w[:, k, cols], x[:, k]) for k in range(DH)
                                    for w, x in ((w_qkv_lo, x_hi[1]), (w_qkv_hi, x_lo[1]), (w_qkv_hi, x_hi[1]))])
                    last.then_inc((km if kind == "k" else qm).sem, 1)
                elif kind == "v":
                    pb = take(it, "B", kind)
                    for t in range(TT):
                        rows = slice(t * P, (t + 1) * P)
                        last = acc(pb[:, t * D:(t + 1) * D],
                                   [(x[:, k, rows], w[:, k, 2 * D:3 * D]) for k in range(DH)
                                    for w, x in ((w_qkv_lo, x_hi[1]), (w_qkv_hi, x_lo[1]), (w_qkv_hi, x_hi[1]))])
                    last.then_inc(vm.sem, 1)
                elif kind == "score":
                    u, b = at
                    g = u // 2
                    if b == 0:
                        kx[u].wait(pe, j, 16 * HU)
                        qc.wait(pe, j, 1)
                    pb = take(it, "B", kind, u, b)
                    if b == 0:
                        q0, k_, m_, n, wid = 0, Kx[:, u % 2, :, 0:P], mask0, HU, P
                    else:
                        q0, k_, m_, n, wid = P, Kx[:, u % 2, 2 * b - 2:2 * b, T - WIN:T], mask1, 2, WIN
                    dst = pb[:, :n * wid].rearrange("p (n w) -> p n w", n=n)
                    nc.tensor.matmul(dst, q_ch[:, g, q0:q0 + P], k_, start=True, stop=False)
                    nc.tensor.matmul(dst, ident_b[:], m_[:].unsqueeze(1).broadcast_to([P, n, wid]),
                                     start=False, stop=True).then_inc(sc.sem, 1)
                elif kind == "ptrans":
                    u, b = at
                    ex.wait(pe, j, 3 * u + min(b + 2, 3))
                    pb = take(it, "B", kind, u, b)
                    if b < 2:
                        src = [x for h in (2 * b, 2 * b + 1) for x in (P0[:, u % 2, h], P1[:, u % 2, h, 0:P])]
                    else:
                        src = [P1[:, u % 2, h, P:T] for h in range(HU)]
                    for n, x in enumerate(src):
                        last = nc.tensor.transpose(pb[:, n * P:(n + 1) * P], x, ident[:])
                    last.then_inc(tt.sem, 1)
                elif kind == "rd":
                    g = at[0]
                    rds.wait(pe, j, 2 * g + 2)
                    pb = take(it, "B", kind, g)
                    for q in range(TT):
                        last = nc.tensor.transpose(pb[:, q * P:(q + 1) * P],
                                                   rden_x[:, q].rearrange("p h c -> p (h c)"), ident[:])
                    last.then_inc(rdt.sem, 1)
                elif kind == "pv":
                    g = at[0]
                    ptd.wait(pe, j, 2 * g + 2)
                    pta.wait(pe, j, 4 * g + 4)
                    vz.wait(pe, j, 2)
                    pb = take(it, "B", kind, g)
                    for pr in range(HG // 2):
                        rows = slice(32 * pr, 32 * pr + 32)
                        for n, h in enumerate((2 * pr, 2 * pr + 1)):
                            u, m = h // HU, h % HU
                            nc.tensor.matmul(pb[rows, 0:T], Vz[:, 0, g * HG + h], PT0[:, u, m],
                                             start=n == 0, stop=False)
                            last = nc.tensor.matmul(pb[rows, P:T], Vz[:, 1, g * HG + h], PT1[:, u, m],
                                                    start=False, stop=n == 1)
                    last.then_inc(pv.sem, 1)
                elif kind == "out_proj":
                    ot.wait(pe, j, DH)
                    pb = take(it, "B", kind)
                    for t in range(TT):
                        last = acc(pb[:, t * D:(t + 1) * D],
                                   [(o_ch[:, k, t * P:(t + 1) * P], w_out[:, k]) for k in range(DH)])
                    last.then_inc(dn[2].sem, 1)

            iterations(pe, "pe", piece)


def kernel(L0_attn_x, L0_attn_A_log, L0_attn_D, L0_attn_x_proj_w, L0_attn_dt_proj_w, L0_attn_dt_proj_b,
           L0_ffn_W_up, L0_ffn_W_gate, L0_ffn_W_down, L1_attn_w_qkv, L1_attn_w_out, L1_ffn_w_gate,
           L1_ffn_w_up, L1_ffn_w_down):
    import numpy as np
    import concourse.bacc as bacc
    from concourse.bass_utils import run_bass_kernel_spmd

    B, S, _ = L0_attn_x.shape
    flip = lambda w: np.ascontiguousarray(np.asarray(w).T)
    xp = np.asarray(L0_attn_x_proj_w)
    bc_rows = xp[P:P + 2 * NS]
    xp = np.concatenate([xp[:P], bc_rows, bc_rows, bc_rows, np.zeros_like(bc_rows)], axis=0)
    arrays = {
        "xT": flip(np.asarray(L0_attn_x).reshape(B * S, D)),
        "A_log": np.ascontiguousarray(L0_attn_A_log),
        "Dskip": flip(np.asarray(L0_attn_D).reshape(DH, P)),
        "xprojT": flip(xp),
        "dtT": flip(L0_attn_dt_proj_w),
        "dt_b": flip(np.asarray(L0_attn_dt_proj_b).reshape(DH, P)),
        "wupT": flip(L0_ffn_W_up),
        "wgateT": flip(L0_ffn_W_gate),
        "wdownT": flip(L0_ffn_W_down),
        "wqkvT": flip(L1_attn_w_qkv),
        "woutT": flip(L1_attn_w_out),
        "wgT2": flip(L1_ffn_w_gate),
        "wuT2": flip(L1_ffn_w_up),
        "wdT2": flip(L1_ffn_w_down),
    }
    nc = bacc.Bacc("TRN2", target_bir_lowering=False, num_devices=1)
    args = [nc.dram_tensor(n, a.shape, mybir.dt.from_np(a.dtype), kind="ExternalInput").ap()
            for n, a in arrays.items()]
    out = nc.dram_tensor("out", (B * S, D), F32, kind="ExternalOutput").ap()
    build(nc, *args, out)
    r = run_bass_kernel_spmd(nc, [arrays], core_ids=[0])
    return r.results[0]["out"].reshape(B, S, D)
```

```python
import concourse.bass as bass
from concourse import mybir
from contextlib import ExitStack

F32 = mybir.dt.float32
F32R = mybir.dt.float32r
BF16 = mybir.dt.bfloat16
ALU = mybir.AluOpType
ACT = mybir.ActivationFunctionType
AX = mybir.AxisListType

P = 128
D = 256
DH = D // P
T = 256
TT = T // P
NS = 16
NP = NS // 2
E = 1024
EK = E // P
H = 16
HC = D // H
HG = H // DH
HU = 4
UNITS = H // HU
WIN = T - 64
LN_EPS = 1e-5
Q_EPS = 1e-8
NEG = -1e30
SCALE = 1.0 / float(HC) ** 0.5
RING = 6
PSUM_COLS = 512

ORDER_TEXT = {
    "pe": """
        -2.A.ffn.0.2 -2.A.ffn.0.3 -2.A.ffn.0.4 -2.A.ffn.0.5 -2.A.ffn.0.6 -2.A.ffn.0.7 -3.B.out_proj
        0.P.xproj -1.S.spread.6 -2.A.down.0 -3.C.turn.2 -1.S.spread.7 0.P.dtproj -3.C.ffn.1.0 -3.C.ffn.1.1
        -2.B.turn.1 -3.C.ffn.1.2 -2.B.k -2.B.q -3.C.ffn.1.3 -3.C.ffn.1.4 0.S.spread.0 -3.C.ffn.1.5 -2.B.v
        0.S.spread.1 -2.B.score.0.0 -2.B.score.0.1 -2.B.score.0.2 -3.C.ffn.1.6 -1.A.turn_in -3.C.ffn.1.7
        -2.B.score.1.0 -2.B.score.1.1 0.S.spread.2 -2.B.score.1.2 -2.B.ptrans.0.0 -2.B.ptrans.0.1
        -2.B.ptrans.0.2 0.S.spread.3 -2.B.score.2.0 -2.B.score.2.1 -2.B.score.2.2 -2.B.ptrans.1.0
        -2.B.ptrans.1.1 -3.C.down.1 0.S.spread.4 -2.B.ptrans.1.2 -2.B.rd.0 -1.A.turn.0 -2.B.score.3.0
        -2.B.score.3.1 -2.B.score.3.2 0.S.spread.5 -2.B.pv.0 -2.B.ptrans.2.0 -2.B.ptrans.2.1 -2.B.ptrans.2.2
        -2.B.ptrans.3.0 -2.B.ptrans.3.1 -2.B.ptrans.3.2 -1.A.ffn.0.0 -1.A.ffn.0.1 -2.B.rd.1 -2.B.pv.1
    """,
    "act": """
        -2.S.spread.4 -4.B.ptrans.1.2 -3.A.turn.0 -4.B.rd.0 -4.B.score.3.0 -4.B.score.3.1 -4.B.score.3.2
        -4.B.ptrans.2.0 -4.B.ptrans.2.2 -4.B.ptrans.3.0 -4.B.ptrans.3.2 -3.A.ffn.0.0 -3.A.ffn.0.1 -4.B.rd.1
        -2.S.spread.5 -3.A.ffn.0.2 -3.A.ffn.0.3 -3.A.high.0 -3.A.ffn.0.4 -3.A.ffn.0.5 -3.A.high.1
        -3.A.ffn.0.6 -3.A.ffn.0.7 -3.A.high.2 -3.A.high.3 -1.P.xproj -2.S.spread.6 -4.C.turn.2 -1.P.dtproj
        -4.C.ffn.1.0 -4.C.ffn.1.1 -3.B.turn.1 -2.S.spread.7 -4.C.ffn.1.2 -3.B.k -3.B.q -4.C.ffn.1.3
        -4.C.ffn.1.4 -1.S.spread.0 -4.C.ffn.1.5 -1.S.spread.1 -3.B.score.0.0 -3.B.score.0.1 -3.B.score.0.2
        -4.C.ffn.1.6 -2.A.turn_in -4.C.ffn.1.7 -1.S.spread.2 -3.B.score.1.0 -3.B.score.1.1 -3.B.score.1.2
        -3.B.ptrans.0.0 -3.B.ptrans.0.2 -1.S.spread.3 -3.B.score.2.0 -3.B.score.2.1 -3.B.score.2.2
        -3.B.ptrans.1.0
    """,
    "dve": """
        0.S.state.7 -2.C.ffn.1.2 +1.S.bound -2.C.ffn.1.3 -2.C.gate.1.2 +1.S.dbu.0 -2.C.gate.1.3 -1.B.q
        -2.C.ffn.1.4 -2.C.gate.1.4 -1.B.v -2.C.ffn.1.5 -1.B.score.0.0 -2.C.gate.1.5 -1.B.score.0.1
        -1.B.score.0.2 +1.S.state.0 +1.S.dbu.1 -2.C.ffn.1.6 -2.C.gate.1.6 -1.B.score.1.0 -1.B.score.1.1
        -2.C.ffn.1.7 -2.C.gate.1.7 +1.S.dbu.2 -1.B.score.1.2 +1.S.state.1 -1.B.ptrans.0.1 0.A.norm.0
        +1.S.state.2 -1.B.score.2.0 -1.B.score.2.1 0.A.aggr.0 +1.S.dbu.3 0.A.eps.0 -1.B.score.2.2
        -1.B.ptrans.1.1 0.A.apply.0 +1.S.state.3 +1.S.dbu.4 -2.C.down.1 -1.B.score.3.0 -1.B.score.3.1
        -1.B.score.3.2 0.A.turn.0 -2.C.norm.3 -2.C.aggr.3 -2.C.eps.3 -1.B.pv.0 -1.B.ptrans.2.1 +1.S.state.4
        -1.B.ptrans.3.1 +1.S.dbu.5 -2.C.apply.3 0.A.ffn.0.0 -1.B.pv.1 0.A.gate.0.0 0.A.ffn.0.1 0.A.gate.0.1
        0.A.ffn.0.2 0.A.ffn.0.3 0.A.gate.0.2 0.A.gate.0.3 0.A.ffn.0.4 0.A.ffn.0.5 0.A.gate.0.4 0.A.gate.0.5
        0.A.ffn.0.6 0.A.ffn.0.7 0.A.gate.0.6 0.A.gate.0.7 -1.B.out_proj -1.B.norm.2 -1.B.aggr.2 -1.B.eps.2
        +1.S.dbu.6 -1.B.apply.2 +2.P.xproj +1.S.state.5 0.A.down.0 0.A.norm.1 0.A.aggr.1 0.A.eps.1
        +2.P.dtproj 0.A.apply.1 +1.S.state.6 -1.C.ffn.1.0 -1.C.ffn.1.1 0.B.turn.1 -1.C.gate.1.0
        -1.C.gate.1.1 +1.S.dbu.7 0.B.k
    """,
    "pool": """
        -3.A.low.0 -3.A.low.1 -3.A.low.2 -3.A.low.3 -4.B.norm.2 -2.S.state.4 -3.A.norm.1 -2.S.state.5
        -2.S.state.6 -2.S.state.7 -1.S.bound -1.S.state.0 -1.S.state.1 -2.A.norm.0 -1.S.state.2 -1.S.state.3
        -4.C.norm.3
    """,
    "sp": """
        -1.P.fetch -3.B.score.0.0 -3.B.score.1.0 -3.B.score.2.0 -3.B.score.3.0 -4.C.apply.3
    """,
}


def pieces_of(text):
    parts = [word.split(".") for word in text.split()]
    return [(int(seq), stage, kind, *map(int, nums)) for seq, stage, kind, *nums in parts]


ORDERS = {engine: pieces_of(text) for engine, text in ORDER_TEXT.items()}
TAKES = ("xproj", "dtproj", "turn_in", "turn", "ffn", "down", "k", "q", "v", "score", "ptrans", "rd", "pv",
         "out_proj")
USES = [p for p in ORDERS["pe"] if p[2] in TAKES]


class Signal:

    def __init__(self, sem, per):
        self.sem, self.per = sem, per

    def wait(self, eng, step, count):
        if isinstance(step, int) and step < 0:
            return
        eng.wait_ge(self.sem, step * self.per + count)


def build(nc, xT, A_log, Dskip, xprojT, dtT, dt_b, wupT, wgateT, wdownT, wqkvT, woutT, wgT2, wuT2, wdT2, out):
    STEPS = xT.shape[1] // T
    with ExitStack() as ctx:
        def sb(name, shape, dt=F32):
            return ctx.enter_context(nc.sbuf_tensor(name, shape, dt))

        w_xp = sb("w_xp", [P, DH, 2 * P])
        w_dt = sb("w_dt", [P, D])
        w_qkv_hi = sb("w_qkv_hi", [P, DH, 3 * D], F32R)
        w_qkv_lo = sb("w_qkv_lo", [P, DH, 3 * D], F32R)
        w_out = sb("w_out", [P, DH, D])
        w_up1 = sb("w_up1", [P, DH, E], F32R)
        w_gate1 = sb("w_gate1", [P, DH, E], F32R)
        w_down1 = sb("w_down1", [P, EK, D], F32R)
        w_gate2 = sb("w_gate2", [P, DH, E])
        w_up2 = sb("w_up2", [P, DH, E])
        w_down2 = sb("w_down2", [P, EK, D])
        ident = sb("ident", [P, P])
        ident_b = sb("ident_b", [P, P], BF16)
        pick = sb("pick", [P, 2 * NS], BF16)
        mask1 = sb("mask1", [P, WIN], BF16)
        mask0 = mask1[:, WIN - P:]
        half_neg = sb("half_neg", [P, TT])
        A_neg = sb("A_neg", [P, DH, NS])
        d_one = sb("d_one", [P, DH])
        b_dt = sb("b_dt", [P, DH])
        q_sum = sb("q_sum", [P, 4])
        q_thr = sb("q_thr", [P, 8])
        x_ch = sb("x_ch", [P, DH, T])
        dr = sb("dr", [P, T])
        z_pos = sb("z_pos", [P, DH, T])
        z_log = sb("z_log", [P, DH, T])
        bc_next = sb("bc_next", [P, T], BF16)
        bc_rest = z_pos[:, 0]
        bc_mid = z_pos[:, 1].bitcast(BF16)[:, 0:T]
        bc_parts = sb("bc_parts", [P, T], BF16)
        delta = sb("delta", [P, DH, T])
        du = sb("du", [P, DH, T])
        dA = sb("dA", [P, 2, 2, DH, T])
        hs = sb("hs", [P, 3, 2, DH, T])
        cs = sb("cs", [P, 2, 2, T])
        r_ch = sb("r_ch", [P, DH, T])
        r_tok = sb("r_tok", [P, TT, D])
        x_tok = [sb(f"x_tok{k}", [P, TT, D]) for k in range(3)]
        x_tok.append(x_tok[2])
        stats = sb("stats", [P, 4, TT, 6])
        mv = sb("mv", [P, 4, TT, 2])
        var_eps = sb("var_eps", [P, 4, TT])
        rstd = sb("rstd", [P, 4, TT])
        pause = sb("pause", [P, 1])
        x_hi = [sb(f"x_hi{k}", [P, DH, T], F32R) for k in range(2)]
        x_lo = [sb(f"x_lo{k}", [P, DH, T], F32R) for k in range(2)]
        x_t = sb("x_t", [P, DH, T])
        th = sb("th", [P, 2, 2, T])
        hid = sb("hid", [P, 2, 2, T])
        at_hidden = nc.sbuf_base
        h_hi = sb("h_hi", [P, EK, T], F32R)
        h_lo = sb("h_lo", [P, EK, T], F32R)
        h2 = sb("h2", [P, EK, T])
        q_hi = sb("q_hi", [P, UNITS, T], F32R)
        q_lo = sb("q_lo", [P, UNITS, T], F32R)
        k_hi = sb("k_hi", [P, DH, T], F32R)
        k_lo = sb("k_lo", [P, DH, T], F32R)
        Kx = sb("Kx", [P, 2, HU, T], F32R)
        Vz = sb("Vz", [P, TT, H, 2 * HC])
        nb = sb("nb", [P, 2, 2, HU])
        den = sb("den", [P, DH, TT, HG])
        rden = sb("rden", [P, TT, HG])
        rden_x = sb("rden_x", [P, TT, HG, HC])
        P0 = sb("P0", [P, 2, HU, P])
        P1 = sb("P1", [P, 2, HU, T])
        at_turned = nc.sbuf_base
        PT0 = sb("PT0", [P, 2, HU, T])
        PT1 = sb("PT1", [P, 2, HU, P])
        rd_ch = sb("rd_ch", [P, T])
        o_ch = sb("o_ch", [P, DH, T])
        ones = nc.alloc_sbuf_tensor_at("ones", [P, P], F32, offset=at_turned + 4 * DH * 3 * D)
        w_raw = nc.alloc_sbuf_tensor_at("w_raw", [P, 3, 2 * E], F32, offset=at_hidden)
        qkv_raw = nc.alloc_sbuf_tensor_at("qkv_raw", [P, DH, 3 * D], F32, offset=at_turned)
        ternary = [w[:].rearrange("p k e -> p (k e)") for w in (w_up1, w_gate1, w_down1)]

        ps = [ctx.enter_context(nc.psum_tensor(f"ps{i}", [P, PSUM_COLS], F32)) for i in range(8)]
        bankB, bankC, ring = ps[0], ps[1], ps[2:]

        def sem(name):
            return ctx.enter_context(nc.semaphore(name))

        def sig(name, per):
            return Signal(sem(name), per)

        s_load = [sem(f"loaded_{n}") for n in range(5)]
        s_const = sem("const_made")
        s_prep = sem("prep_vector")
        s_preps = sem("prep_scalar")
        s_prept = sem("prep_tensor")
        CONST_SCAN, CONST_ONES, CONST_ALL = 6, 11, 19
        PREP_UP_GATE, PREP_ALL = 12, 15
        x_in = sig("x_loaded", 16)
        xdbl = sig("xdbl_made", 1)
        drc = sig("dr_copied", 2)
        bcs = sig("bc_split", 4)
        dtp = sig("dt_made", 1)
        sp = sig("softplus_steps", 3)
        zp = sig("z_positive", 1)
        bd = sig("scan_inputs", 3)
        bb = sig("B_spread", NP)
        bc = sig("C_spread", NP)
        exa = sig("dA_made", NP)
        ccp = sig("C_copied", NP)
        dbu = sig("dBu_made", NP)
        scn = sig("scanned", NP)
        hc = sig("y_steps", 1 + 3 * NP)
        tra = sig("r_turned", 1)
        rtc = sig("r_copied", 1)
        dn = [None] + [sig(f"projected_{k}", 1) for k in (1, 2, 3)]
        rr = [None] + [sig(f"residual_added_{k}", 1) for k in (1, 2, 3)]
        st = [sig(f"stats_steps_{k}", 3) for k in range(4)]
        pw = [sig(f"rstd_made_{k}", 1) for k in range(4)]
        xn = [sig(f"normed_{k}", 1) for k in range(4)]
        trx = [sig(f"x_turned_{k}", 1) for k in range(3)]
        xh = [sig(f"x_high_{k}", 1) for k in range(2)]
        xl = [sig(f"x_low_{k}", 1) for k in range(2)]
        xe = sig("x_copied", 1)
        ug = [sig(f"up_gate_made_{f}", EK) for f in range(2)]
        thd = [sig(f"tanh_made_{f}", EK) for f in range(2)]
        mmd = [sig(f"silu_made_{f}", EK) for f in range(2)]
        hd = [sig(f"hidden_made_{f}", EK) for f in range(2)]
        hh = sig("hidden_high", EK // 2)
        hl = sig("hidden_low", EK // 2)
        qm, km, vm = sig("q_made", 1), sig("k_made", 1), sig("v_made", 1)
        qh, kh = sig("q_high", 1), sig("k_high", 1)
        qc, kc, vz = sig("q_copied", 1), sig("k_copied", 1), sig("v_copied", 2)
        kx = [sig(f"k_spread_{u}", 16 * 2 * HU) for u in range(UNITS)]
        sc = sig("scores_made", 3 * UNITS)
        nbs = sig("max_made", 3 * UNITS)
        ex = sig("exps_made", 3 * UNITS)
        tt = sig("probs_turned", 3 * UNITS)
        ptd = sig("pt_copied_vector", UNITS)
        pta = sig("pt_copied_scalar", 2 * UNITS)
        rds = sig("rden_made", 2 * DH)
        rdt = sig("rden_turned", DH)
        rdc = sig("rden_copied", DH)
        pv = sig("pv_made", DH)
        ot = sig("o_made", DH)
        odma = sig("stored", 16)

        def freed(kind, *at):
            if kind == "xproj":
                return bcs, 1
            if kind == "dtproj":
                return zp, 1
            if kind == "turn_in":
                return rtc, 1
            if kind == "turn":
                return (xl[0], xl[1], xe)[at[0]], 1
            if kind == "ffn":
                return hd[at[0]], at[1] + 1
            if kind == "down":
                return rr[(1, 3)[at[0]]], 1
            if kind == "out_proj":
                return rr[2], 1
            if kind == "score":
                return ex, 3 * at[0] + at[1] + 1
            if kind == "ptrans":
                return (ptd, at[0] + 1) if at[1] == 1 else (pta, 2 * at[0] + 1 + at[1] // 2)
            return {"q": (qc, 1), "k": (kc, 1), "v": (vz, 2), "rd": (rdc, at[0] + 1 if at else 0),
                    "pv": (ot, at[0] + 1 if at else 0)}[kind]

        def use(stage, *piece):
            return [p[1:] for p in USES].index((stage, *piece))

        def bank(stage, *piece):
            return ring[use(stage, *piece) % RING]

        def take(it, stage, *piece, needs=()):
            n = use(stage, *piece)
            slot, held_by, back = n % RING, n - RING, 0
            waits = [(signal, USES[n][0], count) for signal, count in needs]
            while True:
                if held_by < 0:
                    back, held_by = back - 1, max(m for m in range(len(USES)) if m % RING == slot)
                ahead, _, *before = USES[held_by]
                if not isinstance(it, int) or present(it + back + ahead):
                    signal, count = freed(*before)
                    waits.append((signal, back + ahead, count))
                    break
                if it + back < -max(p[0] for p in USES):
                    break
                held_by -= RING
            for signal, rel, count in waits:
                if all(rel * signal.per + count >= r * s.per + c for s, r, c in waits if s is signal):
                    signal.wait(nc.tensor, it + rel, count)
            return ring[slot]

        def present(j):
            return 0 <= j < STEPS

        sums = ring[min(set(range(RING)) - {use(*p) % RING for p in (("P", "xproj"), ("P", "dtproj"),
                                                                      ("A", "turn_in"))})]

        def iterations(eng, which, piece, prepare=None):
            ahead = [p[0] for p in ORDERS[which]]

            def one(it):
                for rel, stage, kind, *at in ORDERS[which]:
                    if isinstance(it, int) and it + rel == 0 and prepare:
                        prepare((stage, kind, *at))
                    if not isinstance(it, int) or present(it + rel):
                        piece(it, it + rel, kind, *at)

            loop = 1 - min(ahead), STEPS - max(ahead)
            for it in range(-max(ahead), loop[0]):
                one(it)
            with eng.Fori(*loop) as it:
                one(it)
            for it in range(loop[1], STEPS - min(ahead)):
                one(it)

        block = ctx.enter_context(nc.Block())

        @block.sync
        def _(sp_):
            def load(dst, src, lot):
                sp_.dma_start(dst, src).then_inc(s_load[lot], 16)

            load(w_xp[:], xprojT.rearrange("(k p) e -> p k e", p=P), 0)
            sp_.dma_start(x_ch[:], xT[:, 0:T].rearrange("(k p) t -> p k t", p=P)).then_inc(x_in.sem, 16)
            load(w_dt[:], dtT, 0)
            load(A_neg[:], A_log.rearrange("(k p) n -> p k n", p=P), 2)
            load(d_one[:], Dskip, 2)
            load(b_dt[:], dt_b, 2)
            for n, (w, rows) in enumerate(((wupT, DH), (wgateT, DH), (wdownT, EK))):
                load(w_raw[:, n, :].rearrange("p (k e) -> p k e", k=rows),
                     w.rearrange("(k p) e -> p k e", p=P), 1)
            load(qkv_raw[:], wqkvT.rearrange("(k p) e -> p k e", p=P), 4)
            for dst, w in ((w_out, woutT), (w_gate2, wgT2), (w_up2, wuT2), (w_down2, wdT2)):
                load(dst[:], w.rearrange("(k p) e -> p k e", p=P), 3)

            def piece(it, j, kind, *at):
                rows = slice(j * T, (j + 1) * T) if isinstance(j, int) else None
                if kind == "fetch" and not (isinstance(j, int) and j == 0):
                    rows = rows or bass.ds(sp_.snap(j * T), T)
                    bd.wait(sp_, j - 1, 3)
                    hc.wait(sp_, j - 1, 1)
                    sp_.dma_start(x_ch[:], xT[:, rows].rearrange("(k p) t -> p k t", p=P)
                                  ).then_inc(x_in.sem, 16)
                elif kind == "score":
                    u = at[0]
                    g, half = divmod(u, 2)
                    if u < 2:
                        kc.wait(sp_, j, 1)
                    else:
                        sc.wait(sp_, j, 3 * (u - 1))
                    for h in range(HU):
                        own = slice((half * HU + h) * HC, (half * HU + h + 1) * HC)
                        for n, part in enumerate((k_hi, k_lo)):
                            to = slice(n * HU * HC + h * HC, n * HU * HC + (h + 1) * HC)
                            sp_.dma_start(Kx[to, u % 2, h, :].bitcast(F32), part[own, g, :].bitcast(F32)
                                          ).then_inc(kx[u].sem, 16)
                elif kind == "apply":
                    rows = rows or bass.ds(sp_.snap(j * T), T)
                    xn[3].wait(sp_, j, 1)
                    sp_.dma_start(out[rows, :].rearrange("(t p) d -> p t d", p=P), x_tok[3][:]
                                  ).then_inc(odma.sem, 16)

            iterations(sp_, "sp", piece)
            odma.wait(sp_, STEPS - 1, 16)

        @block.gpsimd
        def _(pool):
            pool.memset(pick[:], 0.0).then_inc(s_const, 1)
            for c in range(3):
                pool.wait_ge(s_const, 1 + c)
                pool.affine_select(out=pick[:], in_=pick[:], compare_op=ALU.not_equal, fill=1.0, base=-32 * c,
                                   pattern=[[-1, 2 * NS]], channel_multiplier=1).then_inc(s_const, 1)
            for n in range(2):
                pool.memset(dA[:, n, :, :, 0:1], 0.0).then_inc(s_const, 1)
            for t, v in ((ident, 0.0), (ident_b, 0.0), (mask1, 0.0), (half_neg, -0.5), (ones, 1.0)):
                pool.memset(t[:], v).then_inc(s_const, 1)
            pool.wait_ge(s_const, CONST_ONES)
            for t in (ident, ident_b):
                pool.affine_select(out=t[:], in_=t[:], compare_op=ALU.not_equal, fill=1.0, base=0,
                                   pattern=[[-1, P]], channel_multiplier=1).then_inc(s_const, 1)
            pool.affine_select(out=mask1[:], in_=mask1[:], compare_op=ALU.is_ge, fill=NEG, base=64,
                               pattern=[[-1, WIN]], channel_multiplier=1).then_inc(s_const, 1)
            pool.wait_ge(s_const, CONST_ONES + 3)
            pool.affine_select(out=mask1[:], in_=mask1[:], compare_op=ALU.is_ge, fill=NEG, base=0,
                               pattern=[[1, WIN]], channel_multiplier=-1).then_inc(s_const, 1)
            pool.memset(Kx[:].bitcast(F32), 0.0).then_inc(s_const, 1)
            pool.memset(q_lo[:].bitcast(F32), 0.0).then_inc(s_const, 1)
            pool.memset(Vz[:], 0.0).then_inc(s_const, 1)
            pool.memset(P1[:, :, :, 0:T - WIN], 0.0).then_inc(s_const, 1)

            def piece(it, j, kind, *at):
                if kind == "bound":
                    x_in.wait(pool, j, 16)
                    tra.wait(pool, j - 1, 1)
                    pool.tensor_tensor(r_ch[:], x_ch[:], d_one[:].unsqueeze(2).broadcast_to([P, DH, T]),
                                       ALU.mult).then_inc(hc.sem, 1)
                elif kind == "state":
                    n = at[0]
                    scn.wait(pool, j, n + 1)
                    ccp.wait(pool, j, n + 1)
                    pool.tensor_tensor(hs[:, n % 3], hs[:, n % 3],
                                       cs[:, n % 2].unsqueeze(2).broadcast_to([P, 2, DH, T]), ALU.mult
                                       ).then_inc(hc.sem, 1)
                    hc.wait(pool, j, 3 * n + 2)
                    pool.tensor_tensor(r_ch[:], r_ch[:], hs[:, n % 3, 0], ALU.add).then_inc(hc.sem, 1)
                    hc.wait(pool, j, 3 * n + 3)
                    pool.tensor_tensor(r_ch[:], r_ch[:], hs[:, n % 3, 1], ALU.add).then_inc(hc.sem, 1)
                elif kind == "low":
                    pair = at[0]
                    hh.wait(pool, j, pair + 1)
                    dn[1].wait(pool, j - 1, 1)
                    pool.tensor_tensor(h_lo[:, 2 * pair:2 * pair + 2], hid[:, pair % 2],
                                       h_hi[:, 2 * pair:2 * pair + 2].bitcast(F32), ALU.subtract
                                       ).then_inc(hl.sem, 1)
                elif kind == "norm":
                    k = at[0]
                    st[k].wait(pool, j, 3)
                    pool.tensor_tensor(rstd[:, k], var_eps[:, k], half_neg[:], ALU.pow).then_inc(pw[k].sem, 1)

            pool.wait_ge(s_prep, 2)
            iterations(pool, "pool", piece)

        @block.scalar
        def _(act):
            act.wait_ge(s_load[2], 48)
            act.activation(A_neg[:], A_neg[:], ACT.Exp).then_inc(s_preps, 1)

            def prepare(part):
                if part == ("S", "spread", 0):
                    act.wait_ge(s_prep, 1)
                elif part == ("S", "spread", 3):
                    act.wait_ge(s_load[1], 48)
                    for n in range(3):
                        act.activation(ternary[n], w_raw[:, n], ACT.Abs, accum_out=q_sum[:, n:n + 1]
                                       ).then_inc(s_preps, 1)
                elif part == ("A", "turn_in"):
                    act.wait_ge(s_load[4], 16)
                    act.activation(w_qkv_hi[:], qkv_raw[:], ACT.Copy).then_inc(s_preps, 1)
                    act.wait_ge(s_const, CONST_ALL)
                elif part == ("A", "ffn", 0, 0):
                    act.wait_ge(s_prep, PREP_UP_GATE)

            def piece(it, j, kind, *at):
                if kind == "xproj":
                    pb = bank("P", kind)
                    xdbl.wait(act, j, 1)
                    act.activation(dr[:], pb[:, 0:T], ACT.Copy).then_inc(drc.sem, 1)
                    bd.wait(act, j - 1, 1)
                    act.activation(bc_next[:], pb[:, T:2 * T], ACT.Copy).then_inc(drc.sem, 1)
                elif kind == "dtproj":
                    dtp.wait(act, j, 1)
                    bd.wait(act, j - 1, 2)
                    for h in range(DH):
                        last = act.activation(z_log[:, h], bank("P", kind)[:, h * T:(h + 1) * T], ACT.Abs,
                                              bias=b_dt[:, h:h + 1])
                    last.then_inc(sp.sem, 1)
                    sp.wait(act, j, 1)
                    act.activation(z_log[:], z_log[:], ACT.Exp, scale=-1.0).then_inc(sp.sem, 1)
                    sp.wait(act, j, 2)
                    act.activation(z_log[:], z_log[:], ACT.Ln, bias=1.0).then_inc(sp.sem, 1)
                elif kind == "spread":
                    n = at[0]
                    if n == 0:
                        bd.wait(act, j, 2)
                    if n >= 2:
                        scn.wait(act, j, n - 1)
                    else:
                        scn.wait(act, j - 1, NP - 1 + n)
                    for m in range(2):
                        for h in range(DH):
                            last = act.activation(dA[:, n % 2, m, h, 1:], delta[:, h, 1:], ACT.Exp,
                                                  scale=A_neg[:, h, 2 * n + m:2 * n + m + 1])
                    last.then_inc(exa.sem, 1)
                    bc.wait(act, j, n + 1)
                    if n >= 2:
                        hc.wait(act, j, 3 * (n - 2) + 2)
                    else:
                        hc.wait(act, j - 1, 3 * (NP - 2 + n) + 2)
                    act.activation(cs[:, n % 2].rearrange("p m t -> p (m t)"), bankC[:], ACT.Copy
                                   ).then_inc(ccp.sem, 1)
                elif kind == "turn_in":
                    tra.wait(act, j, 1)
                    xn[0].wait(act, j - 1, 1)
                    act.activation(r_tok[:].rearrange("p t d -> p (t d)"), bank("A", kind)[:], ACT.Copy
                                   ).then_inc(rtc.sem, 1)
                elif kind == "turn":
                    k = at[0]
                    src = bank("ABC"[k], kind, k)[:]
                    trx[k].wait(act, j, 1)
                    if k < 2:
                        act.activation(x_hi[k][:].rearrange("p k t -> p (k t)"), src, ACT.Copy
                                       ).then_inc(xh[k].sem, 1)
                    else:
                        act.activation(x_t[:].rearrange("p k t -> p (k t)"), src, ACT.Copy
                                       ).then_inc(xe.sem, 1)
                elif kind == "ffn":
                    f, e = at
                    ug[f].wait(act, j, e + 1)
                    if e >= 2:
                        hd[f].wait(act, j, e - 1)
                    act.activation(th[:, f, e % 2], bank("AC"[f], kind, f, e)[:, 0:T], ACT.Tanh,
                                   scale=q_thr[:, 6:7] if f == 0 else 0.5).then_inc(thd[f].sem, 1)
                elif kind == "high":
                    pair = at[0]
                    hd[0].wait(act, j, 2 * pair + 2)
                    dn[1].wait(act, j - 1, 1)
                    act.activation(h_hi[:, 2 * pair:2 * pair + 2], hid[:, pair % 2], ACT.Copy
                                   ).then_inc(hh.sem, 1)
                elif kind == "q":
                    qm.wait(act, j, 1)
                    sc.wait(act, j - 1, 3 * UNITS)
                    for half in range(2):
                        src = bank("B", kind)[64 * half:64 * half + 64, :].rearrange("p (g t) -> p g t", g=DH)
                        for rows in (slice(0, 64), slice(64, P)):
                            last = act.activation(q_hi[rows, half::2, :], src, ACT.Copy, scale=SCALE)
                    last.then_inc(qh.sem, 1)
                elif kind == "k":
                    km.wait(act, j, 1)
                    sc.wait(act, j - 1, 3 * UNITS)
                    act.activation(k_hi[:].rearrange("p k t -> p (k t)"), bank("B", kind)[:], ACT.Copy
                                   ).then_inc(kh.sem, 1)
                elif kind == "score":
                    u, b = at
                    g, half = divmod(u, 2)
                    nbs.wait(act, j, 3 * u + b + 1)
                    if b == 0 and u >= 2:
                        tt.wait(act, j, 3 * (u - 1))
                    q, heads, wid = (0, range(HU), P) if b == 0 else (1, range(2 * b - 2, 2 * b), WIN)
                    for n, h in enumerate(heads):
                        dst = P0[:, u % 2, h] if b == 0 else P1[:, u % 2, h, T - WIN:T]
                        last = act.activation(dst, bank("B", kind, u, b)[:, n * wid:(n + 1) * wid], ACT.Exp,
                                              bias=nb[:, u % 2, q, h:h + 1],
                                              accum_out=den[:, g, q, half * HU + h:half * HU + h + 1])
                    last.then_inc(ex.sem, 1)
                elif kind == "ptrans" and at[1] != 1:
                    u, b = at
                    tt.wait(act, j, 3 * u + b + 1)
                    if u >= 2 and b == 0:
                        pv.wait(act, j, 1)
                    dst = PT0[:, u % 2, 0:2] if b == 0 else PT1[:, u % 2]
                    act.activation(dst.rearrange("p a b -> p (a b)"), bank("B", kind, u, b)[:], ACT.Copy
                                   ).then_inc(pta.sem, 1)
                elif kind == "rd":
                    g = at[0]
                    rdt.wait(act, j, g + 1)
                    if g:
                        ot.wait(act, j, g)
                    act.activation(rd_ch[:], bank("B", kind, g)[:, 0:T], ACT.Copy).then_inc(rdc.sem, 1)

            iterations(act, "act", piece, prepare)

        @block.vector
        def _(dve):
            dve.wait_ge(s_preps, 1)
            dve.tensor_scalar(A_neg[:], A_neg[:], -1.0, None, ALU.mult).then_inc(s_prep, 1)
            dve.tensor_scalar(d_one[:], d_one[:], 1.0, None, ALU.add).then_inc(s_prep, 1)

            def prepare(part):
                if part == ("S", "dbu", 0):
                    dve.wait_ge(s_const, CONST_SCAN)
                elif part == ("S", "state", 3):
                    dve.wait_ge(s_prept, 1)
                    dve.tensor_scalar(q_sum[:, 0:3], sums[:, 0:3], 1.0 / (D * E), Q_EPS, ALU.mult, ALU.add
                                      ).then_inc(s_prep, 1)
                    dve.wait_ge(s_prep, 3)
                    dve.tensor_scalar(q_thr[:, 0:3], q_sum[:, 0:3], 0.5, None, ALU.mult).then_inc(s_prep, 1)
                    dve.tensor_scalar(q_thr[:, 3:6], q_sum[:, 0:3], -0.5, None, ALU.mult).then_inc(s_prep, 1)
                    dve.wait_ge(s_prep, 5)
                    dve.tensor_scalar(q_thr[:, 6:7], q_thr[:, 0:1], 1.0, None, ALU.mult).then_inc(s_prep, 1)
                    dve.tensor_tensor(q_thr[:, 7:8], q_thr[:, 0:1], q_sum[:, 1:2], ALU.mult
                                      ).then_inc(s_prep, 1)
                    dve.wait_ge(s_prep, 7)
                    dve.tensor_tensor(q_thr[:, 7:8], q_thr[:, 7:8], q_sum[:, 2:3], ALU.mult
                                      ).then_inc(s_prep, 1)
                    to_ternary(0)
                elif part == ("S", "state", 4):
                    to_ternary(1)
                elif part == ("A", "norm", 0):
                    to_ternary(2)
                    dve.wait_ge(s_preps, 5)
                    dve.tensor_tensor(w_qkv_lo[:], qkv_raw[:], w_qkv_hi[:].bitcast(F32), ALU.subtract
                                      ).then_inc(s_prep, 1)
                    dve.wait_ge(s_prep, PREP_ALL)
                    dve.wait_ge(s_const, CONST_ALL)

            def to_ternary(n):
                dve.tensor_scalar(ternary[n], w_raw[:, n], q_thr[:, 3 + n:4 + n], None, ALU.is_lt
                                  ).then_inc(s_prep, 1)
                dve.wait_ge(s_prep, 9 + 2 * n)
                dve.scalar_tensor_tensor(ternary[n], w_raw[:, n], q_thr[:, n:n + 1], ternary[n].bitcast(F32),
                                         ALU.is_gt, ALU.subtract).then_inc(s_prep, 1)

            def piece(it, j, kind, *at):
                if kind == "xproj":
                    drc.wait(dve, j, 2)
                    bd.wait(dve, j - 1, 2)
                    dve.tensor_tensor(bc_rest[:], bank("P", kind)[:, T:2 * T], bc_next[:], ALU.subtract
                                      ).then_inc(bcs.sem, 1)
                    bcs.wait(dve, j, 1)
                    dve.tensor_copy(bc_next[32:64], bc_rest[32:64]).then_inc(bcs.sem, 1)
                    dve.tensor_copy(bc_mid[64:96], bc_rest[64:96]).then_inc(bcs.sem, 1)
                    bcs.wait(dve, j, 3)
                    dve.tensor_tensor(bc_next[64:96], bc_rest[64:96], bc_mid[64:96], ALU.subtract
                                      ).then_inc(bcs.sem, 1)
                elif kind == "dtproj":
                    sp.wait(dve, j, 1)
                    bcs.wait(dve, j, 4)
                    for h in range(DH):
                        last = dve.tensor_scalar(z_pos[:, h], bank("P", kind)[:, h * T:(h + 1) * T],
                                                 b_dt[:, h:h + 1], 0.0, ALU.add, ALU.max)
                    last.then_inc(zp.sem, 1)
                elif kind == "bound":
                    bcs.wait(dve, j, 4)
                    bb.wait(dve, j - 1, NP)
                    bc.wait(dve, j - 1, NP)
                    dve.tensor_copy(bc_parts[:], bc_next[:]).then_inc(bd.sem, 1)
                    sp.wait(dve, j, 3)
                    zp.wait(dve, j, 1)
                    exa.wait(dve, j - 1, NP)
                    dve.tensor_tensor(delta[:], z_pos[:], z_log[:], ALU.add).then_inc(bd.sem, 1)
                    bd.wait(dve, j, 2)
                    x_in.wait(dve, j, 16)
                    dve.tensor_tensor(du[:], delta[:], x_ch[:], ALU.mult).then_inc(bd.sem, 1)
                elif kind == "dbu":
                    n = at[0]
                    if n == 0:
                        bd.wait(dve, j, 3)
                    bb.wait(dve, j, n + 1)
                    if n >= 3:
                        hc.wait(dve, j, 3 * (n - 2) + 1)
                    else:
                        last = max(m for m in range(NP) if m % 3 == n)
                        hc.wait(dve, j - 1, 3 * (last + 1) + 1)
                    dve.tensor_tensor(hs[:, n % 3], du[:].unsqueeze(1).broadcast_to([P, 2, DH, T]),
                                      bankB[:].rearrange("p (m t) -> p m t", m=2).unsqueeze(2)
                                      .broadcast_to([P, 2, DH, T]), ALU.mult).then_inc(dbu.sem, 1)
                elif kind == "state":
                    n = at[0]
                    dbu.wait(dve, j, n + 1)
                    exa.wait(dve, j, n + 1)
                    flat = hs[:, n % 3].rearrange("p m h t -> p (m h t)")
                    dve.tensor_tensor_scan(flat, dA[:, n % 2].rearrange("p m h t -> p (m h t)"), flat, 0.0,
                                           ALU.mult, ALU.add).then_inc(scn.sem, 1)
                elif kind == "norm":
                    k = at[0]
                    if k:
                        rr[k].wait(dve, j, 1)
                    else:
                        rtc.wait(dve, j, 1)
                    for t in range(TT):
                        last = dve.bn_stats(stats[:, k, t], rows_in(k, t))
                    last.then_inc(st[k].sem, 1)
                elif kind == "aggr":
                    k = at[0]
                    st[k].wait(dve, j, 1)
                    dve.memset(pause[:], 0.0)
                    for t in range(TT):
                        last = dve.bn_aggr(mv[:, k, t], stats[:, k, t])
                    last.then_inc(st[k].sem, 1)
                elif kind == "eps":
                    k = at[0]
                    st[k].wait(dve, j, 2)
                    dve.tensor_scalar(var_eps[:, k], mv[:, k, :, 1], LN_EPS, None, ALU.add
                                      ).then_inc(st[k].sem, 1)
                elif kind == "apply":
                    k = at[0]
                    pw[k].wait(dve, j, 1)
                    if k < 2:
                        xn[k + 1].wait(dve, j - 1, 1)
                    elif k == 2:
                        odma.wait(dve, j - 1, 16)
                    for t in range(TT):
                        last = dve.tensor_scalar(x_tok[k][:, t], rows_in(k, t), mv[:, k, t, 0:1],
                                                 rstd[:, k, t:t + 1], ALU.subtract, ALU.mult)
                    last.then_inc(xn[k].sem, 1)
                elif kind == "turn" and at[0] < 2:
                    k = at[0]
                    xh[k].wait(dve, j, 1)
                    dve.tensor_tensor(x_lo[k][:].rearrange("p k t -> p (k t)"), bank("AB"[k], kind, k)[:],
                                      x_hi[k][:].rearrange("p k t -> p (k t)").bitcast(F32), ALU.subtract
                                      ).then_inc(xl[k].sem, 1)
                elif kind == "ffn":
                    f, e = at
                    pb = bank("AC"[f], kind, f, e)
                    thd[f].wait(dve, j, e + 1)
                    m = th[:, f, e % 2]
                    dve.scalar_tensor_tensor(m, m, 1.0, pb[:, 0:T], ALU.add, ALU.mult).then_inc(mmd[f].sem, 1)
                elif kind == "gate":
                    f, e = at
                    pb, m = bank("AC"[f], "ffn", f, e), th[:, f, e % 2]
                    mmd[f].wait(dve, j, e + 1)
                    if f == 1 and e == 0:
                        dn[3].wait(dve, j - 1, 1)
                    if f == 0 and e % 2 == 0:
                        hl.wait(dve, *((j, e // 2 - 1) if e >= 4 else (j - 1, (EK + e) // 2 - 1)))
                    dst = hid[:, (e // 2) % 2, e % 2] if f == 0 else h2[:, e]
                    dve.tensor_tensor(dst, m, pb[:, T:2 * T], ALU.mult).then_inc(hd[f].sem, 1)
                elif kind in ("down", "out_proj"):
                    stage, k = {("down", 0): ("A", 1), ("out_proj",): ("B", 2), ("down", 1): ("C", 3)}[(kind, *at)]
                    x = x_tok[k - 1][:].rearrange("p a b -> p (a b)")
                    dn[k].wait(dve, j, 1)
                    dve.scalar_tensor_tensor(x, bank(stage, kind, *at)[:], (q_thr[:, 7:8], 1.0, 0.5)[k - 1], x,
                                             ALU.mult, ALU.add).then_inc(rr[k].sem, 1)
                elif kind == "k":
                    kh.wait(dve, j, 1)
                    dve.tensor_tensor(k_lo[:].rearrange("p k t -> p (k t)"), bank("B", kind)[:],
                                      k_hi[:].rearrange("p k t -> p (k t)").bitcast(F32), ALU.subtract
                                      ).then_inc(kc.sem, 1)
                elif kind == "q":
                    qh.wait(dve, j, 1)
                    for half in range(2):
                        rows = slice(64 * half, 64 * half + 64)
                        last = dve.scalar_tensor_tensor(
                            q_lo[0:64, half::2, :], bank("B", kind)[rows, :].rearrange("p (g t) -> p g t", g=DH),
                            SCALE, q_hi[rows, half::2, :].bitcast(F32), ALU.mult, ALU.subtract)
                    last.then_inc(qc.sem, 1)
                elif kind == "v":
                    vm.wait(dve, j, 1)
                    dst = Vz[:].rearrange("p t (a o) d -> p t a o d", o=2)
                    src = bank("B", kind)[:].rearrange("p (t a o d) -> p t a o d", t=TT, a=H // 2, o=2)
                    for odd in range(2):
                        dve.tensor_copy(dst[:, :, :, odd, HC * odd:HC * odd + HC], src[:, :, :, odd, :]
                                        ).then_inc(vz.sem, 1)
                elif kind == "score":
                    u, b = at
                    sc.wait(dve, j, 3 * u + b + 1)
                    q, h0, n, wid = (0, 0, HU, P) if b == 0 else (1, 2 * b - 2, 2, WIN)
                    if b == 0:
                        ex.wait(dve, *((j, 3 * (u - 1)) if u >= 2 else (j - 1, 3 * (UNITS - 1 + u))))
                    dve.tensor_reduce(nb[:, u % 2, q, h0:h0 + n],
                                      bank("B", kind, u, b)[:, :n * wid].rearrange("p (n w) -> p n w", n=n),
                                      AX.X, ALU.max, negate=True).then_inc(nbs.sem, 1)
                elif kind == "ptrans" and at[1] == 1:
                    u = at[0]
                    tt.wait(dve, j, 3 * u + 2)
                    if u >= 2:
                        pv.wait(dve, j, 1)
                    dve.tensor_copy(PT0[:, u % 2, 2:4].rearrange("p a b -> p (a b)"),
                                    bank("B", kind, u, 1)[:]).then_inc(ptd.sem, 1)
                    if u % 2:
                        g = u // 2
                        dve.reciprocal(rden[:].rearrange("p q h -> p (q h)"),
                                       den[:, g].rearrange("p q h -> p (q h)")).then_inc(rds.sem, 1)
                        rds.wait(dve, j, 2 * g + 1)
                        rdt.wait(dve, *((j, g) if g else (j - 1, DH)))
                        dve.tensor_copy(rden_x[:].rearrange("p q h c -> p (q h) c"),
                                        rden[:].rearrange("p q h -> p (q h)").unsqueeze(2)
                                        .broadcast_to([P, TT * HG, HC])).then_inc(rds.sem, 1)
                elif kind == "pv":
                    g = at[0]
                    rdc.wait(dve, j, g + 1)
                    pv.wait(dve, j, g + 1)
                    dve.tensor_tensor(o_ch[:, g], bank("B", kind, g)[:, 0:T], rd_ch[:], ALU.mult
                                      ).then_inc(ot.sem, 1)

            def rows_in(k, t):
                return (r_tok if k == 0 else x_tok[k - 1])[:, t]

            iterations(dve, "dve", piece, prepare)

        @block.tensor
        def _(pe):
            pe.wait_ge(s_load[0], 32)

            def prepare(part):
                if part == ("S", "spread", 0):
                    pe.wait_ge(s_const, CONST_SCAN)
                elif part == ("S", "spread", 4):
                    pe.wait_ge(s_preps, 4)
                    pe.wait_ge(s_const, CONST_ONES)
                    nc.tensor.matmul(sums[:, 0:3], ones[:], q_sum[:, 0:3], start=True, stop=True
                                     ).then_inc(s_prept, 1)
                elif part == ("A", "turn_in"):
                    pe.wait_ge(s_load[3], 64)
                    pe.wait_ge(s_const, CONST_ALL)
                elif part == ("A", "ffn", 0, 0):
                    pe.wait_ge(s_prep, PREP_UP_GATE)
                elif part == ("A", "down", 0):
                    pe.wait_ge(s_prep, PREP_ALL)

            def acc(dst, pairs):
                for n, (l, r) in enumerate(pairs):
                    last = nc.tensor.matmul(dst, l, r, start=n == 0, stop=n == len(pairs) - 1)
                return last

            def piece(it, j, kind, *at):
                if kind == "xproj":
                    pb = take(it, "P", kind, needs=[(x_in, 16)])
                    for m in range(2):
                        last = acc(pb[:, m * T:(m + 1) * T],
                                   [(w_xp[:, k, m * P:(m + 1) * P], x_ch[:, k]) for k in range(DH)])
                    last.then_inc(xdbl.sem, 1)
                elif kind == "dtproj":
                    pb = take(it, "P", kind, needs=[(drc, 1)])
                    for h in range(DH):
                        last = acc(pb[:, h * T:(h + 1) * T], [(w_dt[:, h * P:(h + 1) * P], dr[:])])
                    last.then_inc(dtp.sem, 1)
                elif kind == "spread":
                    n = at[0]
                    if n == 0:
                        bd.wait(pe, j, 1)
                    for base, dst, used, done in ((0, bankB, dbu, bb), (NS, bankC, ccp, bc)):
                        used.wait(pe, *((j, n) if n else (j - 1, NP)))
                        for m in range(2):
                            row = base + 2 * n + m
                            last = nc.tensor.matmul(dst[:, m * T:(m + 1) * T],
                                                    pick[:, row:row + 1].broadcast_to([P, P]), bc_parts[:],
                                                    start=True, stop=True)
                        last.then_inc(done.sem, 1)
                elif kind == "turn_in":
                    pb = take(it, "A", kind, needs=[(hc, 3 * NP + 1)])
                    for t in range(TT):
                        for c in range(DH):
                            last = nc.tensor.transpose(pb[:, t * D + c * P:t * D + (c + 1) * P],
                                                       r_ch[:, c, t * P:(t + 1) * P], ident[:])
                    last.then_inc(tra.sem, 1)
                elif kind == "turn":
                    k = at[0]
                    pb = take(it, "ABC"[k], kind, k, needs=[(xn[k], 1)])
                    for c in range(DH):
                        for t in range(TT):
                            last = nc.tensor.transpose(pb[:, c * T + t * P:c * T + (t + 1) * P],
                                                       x_tok[k][:, t, c * P:(c + 1) * P], ident[:])
                    last.then_inc(trx[k].sem, 1)
                elif kind == "ffn":
                    f, e = at
                    pb = take(it, "AC"[f], kind, f, e, needs=[((xl[0], xe)[f], 1)] if e == 0 else ())
                    cols = slice(e * P, (e + 1) * P)
                    for n in range(2):
                        if f == 0:
                            w = (w_up1, w_gate1)[n]
                            pairs = [(w[:, k, cols], x[:, k]) for k in range(DH) for x in (x_lo[0], x_hi[0])]
                        else:
                            w = (w_gate2, w_up2)[n]
                            pairs = [(w[:, k, cols], x_t[:, k]) for k in range(DH)]
                        last = acc(pb[:, n * T:(n + 1) * T], pairs)
                    last.then_inc(ug[f].sem, 1)
                elif kind == "down":
                    f = at[0]
                    pb = take(it, "AC"[f], kind, f, needs=[((hl, EK // 2), (hd[1], EK))[f]])
                    for t in range(TT):
                        rows = slice(t * P, (t + 1) * P)
                        if f == 0:
                            pairs = [(x[:, e, rows], w_down1[:, e]) for e in range(EK) for x in (h_lo, h_hi)]
                        else:
                            pairs = [(h2[:, e, rows], w_down2[:, e]) for e in range(EK)]
                        last = acc(pb[:, t * D:(t + 1) * D], pairs)
                    last.then_inc(dn[(1, 3)[f]].sem, 1)
                elif kind in ("q", "k"):
                    pb = take(it, "B", kind, needs=[(xl[1], 1)] if kind == "k" else ())
                    for g in range(DH):
                        cols = slice((D if kind == "k" else 0) + g * P, (D if kind == "k" else 0) + (g + 1) * P)
                        last = acc(pb[:, g * T:(g + 1) * T],
                                   [(w[:, k, cols], x[:, k]) for k in range(DH)
                                    for w, x in ((w_qkv_lo, x_hi[1]), (w_qkv_hi, x_lo[1]), (w_qkv_hi, x_hi[1]))])
                    last.then_inc((km if kind == "k" else qm).sem, 1)
                elif kind == "v":
                    pb = take(it, "B", kind)
                    for t in range(TT):
                        rows = slice(t * P, (t + 1) * P)
                        last = acc(pb[:, t * D:(t + 1) * D],
                                   [(x[:, k, rows], w[:, k, 2 * D:3 * D]) for k in range(DH)
                                    for w, x in ((w_qkv_lo, x_hi[1]), (w_qkv_hi, x_lo[1]), (w_qkv_hi, x_hi[1]))])
                    last.then_inc(vm.sem, 1)
                elif kind == "score":
                    u, b = at
                    pb = take(it, "B", kind, u, b,
                              needs=[(kx[u], 16 * 2 * HU), (qc, 1)] if b == 0 else ())
                    if b == 0:
                        q0, k_, m_, n, wid = 0, Kx[:, u % 2, :, 0:P], mask0, HU, P
                    else:
                        q0, k_, m_, n, wid = P, Kx[:, u % 2, 2 * b - 2:2 * b, T - WIN:T], mask1, 2, WIN
                    dst = pb[:, :n * wid].rearrange("p (n w) -> p n w", n=n)
                    nc.tensor.matmul(dst, q_lo[:, u, q0:q0 + P], k_, start=True, stop=False)
                    nc.tensor.matmul(dst, q_hi[:, u, q0:q0 + P], k_, start=False, stop=False)
                    nc.tensor.matmul(dst, ident_b[:], m_[:].unsqueeze(1).broadcast_to([P, n, wid]),
                                     start=False, stop=True).then_inc(sc.sem, 1)
                elif kind == "ptrans":
                    u, b = at
                    pb = take(it, "B", kind, u, b, needs=[(ex, 3 * u + min(b + 2, 3))])
                    if b < 2:
                        src = [x for h in (2 * b, 2 * b + 1) for x in (P0[:, u % 2, h], P1[:, u % 2, h, 0:P])]
                    else:
                        src = [P1[:, u % 2, h, P:T] for h in range(HU)]
                    for n, x in enumerate(src):
                        last = nc.tensor.transpose(pb[:, n * P:(n + 1) * P], x, ident[:])
                    last.then_inc(tt.sem, 1)
                elif kind == "rd":
                    g = at[0]
                    pb = take(it, "B", kind, g, needs=[(rds, 2 * g + 2)])
                    for q in range(TT):
                        last = nc.tensor.transpose(pb[:, q * P:(q + 1) * P],
                                                   rden_x[:, q].rearrange("p h c -> p (h c)"), ident[:])
                    last.then_inc(rdt.sem, 1)
                elif kind == "pv":
                    g = at[0]
                    pb = take(it, "B", kind, g, needs=[(ptd, 2 * g + 2), (pta, 4 * g + 4), (vz, 2)])
                    for pr in range(HG // 2):
                        rows = slice(32 * pr, 32 * pr + 32)
                        for n, h in enumerate((2 * pr, 2 * pr + 1)):
                            u, m = h // HU, h % HU
                            nc.tensor.matmul(pb[rows, 0:T], Vz[:, 0, g * HG + h], PT0[:, u, m],
                                             start=n == 0, stop=False)
                            last = nc.tensor.matmul(pb[rows, P:T], Vz[:, 1, g * HG + h], PT1[:, u, m],
                                                    start=False, stop=n == 1)
                    last.then_inc(pv.sem, 1)
                elif kind == "out_proj":
                    pb = take(it, "B", kind, needs=[(ot, DH)])
                    for t in range(TT):
                        last = acc(pb[:, t * D:(t + 1) * D],
                                   [(o_ch[:, k, t * P:(t + 1) * P], w_out[:, k]) for k in range(DH)])
                    last.then_inc(dn[2].sem, 1)

            iterations(pe, "pe", piece, prepare)


def kernel(L0_attn_x, L0_attn_A_log, L0_attn_D, L0_attn_x_proj_w, L0_attn_dt_proj_w, L0_attn_dt_proj_b,
           L0_ffn_W_up, L0_ffn_W_gate, L0_ffn_W_down, L1_attn_w_qkv, L1_attn_w_out, L1_ffn_w_gate,
           L1_ffn_w_up, L1_ffn_w_down):
    import numpy as np
    import concourse.bacc as bacc
    from concourse.bass_utils import run_bass_kernel_spmd

    B, S, _ = L0_attn_x.shape
    flip = lambda w: np.ascontiguousarray(np.asarray(w).T)
    xp = np.asarray(L0_attn_x_proj_w)
    bc_rows = xp[P:P + 2 * NS]
    xp = np.concatenate([xp[:P], bc_rows, bc_rows, bc_rows, np.zeros_like(bc_rows)], axis=0)
    arrays = {
        "xT": flip(np.asarray(L0_attn_x).reshape(B * S, D)),
        "A_log": np.ascontiguousarray(L0_attn_A_log),
        "Dskip": flip(np.asarray(L0_attn_D).reshape(DH, P)),
        "xprojT": flip(xp),
        "dtT": flip(L0_attn_dt_proj_w),
        "dt_b": flip(np.asarray(L0_attn_dt_proj_b).reshape(DH, P)),
        "wupT": flip(L0_ffn_W_up),
        "wgateT": flip(L0_ffn_W_gate),
        "wdownT": flip(L0_ffn_W_down),
        "wqkvT": flip(L1_attn_w_qkv),
        "woutT": flip(L1_attn_w_out),
        "wgT2": flip(L1_ffn_w_gate),
        "wuT2": flip(L1_ffn_w_up),
        "wdT2": flip(L1_ffn_w_down),
    }
    nc = bacc.Bacc("TRN2", target_bir_lowering=False, num_devices=1)
    args = [nc.dram_tensor(n, a.shape, mybir.dt.from_np(a.dtype), kind="ExternalInput").ap()
            for n, a in arrays.items()]
    out = nc.dram_tensor("out", (B * S, D), F32, kind="ExternalOutput").ap()
    build(nc, *args, out)
    r = run_bass_kernel_spmd(nc, [arrays], core_ids=[0])
    return r.results[0]["out"].reshape(B, S, D)
```
